# Optimizing a Trainium2 kernel written in Bass

```python
import numpy as np
import jax
import jax.numpy as jnp

def _softmax(x, axis=-1):
    return jax.nn.softmax(x, axis=axis)

def _gelu(x):
    return jax.nn.gelu(x, approximate=True)

def _silu(x):
    return jax.nn.silu(x)

def _sigmoid(x):
    return jax.nn.sigmoid(x)

def _layernorm(x, axis=-1, eps=1e-05):
    m = jnp.mean(x, axis=axis, keepdims=True)
    v = jnp.var(x, axis=axis, keepdims=True)
    return (x - m) / jnp.sqrt(v + eps)

def _scatter_add(tgt, idx, src, axis=0):
    return tgt.at[idx].add(src)

def _segment_sum(src, seg, n):
    return jax.ops.segment_sum(src, seg, n)
kernel_name = 'mk_hybrid_d1_jaxref_r8_80ab53'

def setup_inputs(seed: int=0):
    np.random.seed(seed)
    _w = jnp.asarray

    def _L0_attn_a_setup():
        import jax, jax.numpy as jnp
        import numpy as np
        D_MODEL = 128
        N_HEADS = 16
        HEAD_DIM = D_MODEL // N_HEADS
        ROPE_THETA = 10000.0
        EPS = 1e-06
        PAD_VAL = 1.0

        def _rope(x, cos, sin):
            x1 = x[..., 0::2]
            x2 = x[..., 1::2]
            r1 = x1 * cos - x2 * sin
            r2 = x1 * sin + x2 * cos
            return jnp.stack([r1, r2], axis=-1).reshape(x.shape)
        key = jax.random.key(seed)
        ks = jax.random.split(key, 5)
        w_scale = 1.0 / np.sqrt(D_MODEL)
        return {'x': jax.random.normal(ks[0], (4, 512, D_MODEL), jnp.float32), 'Wq': jax.random.normal(ks[1], (D_MODEL, D_MODEL), jnp.float32) * w_scale, 'Wk': jax.random.normal(ks[2], (D_MODEL, D_MODEL), jnp.float32) * w_scale, 'Wv': jax.random.normal(ks[3], (D_MODEL, D_MODEL), jnp.float32) * w_scale, 'Wo': jax.random.normal(ks[4], (D_MODEL, D_MODEL), jnp.float32) * w_scale}
    _L0_attn_a_in = _L0_attn_a_setup()

    def _L0_attn_b_setup():
        import jax, jax.numpy as jnp
        import numpy as np
        from jax import lax
        B, S, E, SD = (8, 512, 128, 8)

        def _reference_tuple_inner(x, W_in, b_in, W_g, b_g, W_out, b_out):
            embed_dim = W_in.shape[0]
            combined = jnp.einsum('bse,ec->bsc', x, W_in) + b_in
            embed = combined[..., :embed_dim]
            state_in = combined[..., embed_dim:]
            gate = jax.nn.sigmoid(jnp.einsum('bsc,cd->bsd', combined, W_g) + b_g)

            def step(state, gs):
                g, si = gs
                new = g * state + (1.0 - g) * si
                return (new, new)
            state0 = jnp.zeros((x.shape[0], state_in.shape[-1]), dtype=x.dtype)
            g_t = jnp.moveaxis(gate, 1, 0)
            si_t = jnp.moveaxis(state_in, 1, 0)
            final_state, states = lax.scan(step, state0, (g_t, si_t))
            states = jnp.moveaxis(states, 0, 1)
            out = jnp.einsum('bsc,cd->bsd', jnp.concatenate([embed, states], axis=-1), W_out) + b_out
            return (out, final_state)
        key = jax.random.key(seed)
        ks = jax.random.split(key, 4)
        x = jax.random.normal(ks[0], (B, S, E), dtype=jnp.float32)
        W_in = jax.random.normal(ks[1], (E, E + SD), dtype=jnp.float32) / np.sqrt(E)
        b_in = jnp.zeros((E + SD,), dtype=jnp.float32)
        W_g = jax.random.normal(ks[2], (E + SD, SD), dtype=jnp.float32) / np.sqrt(E + SD)
        b_g = jnp.zeros((SD,), dtype=jnp.float32)
        W_out = jax.random.normal(ks[3], (E + SD, E), dtype=jnp.float32) / np.sqrt(E + SD)
        b_out = jnp.zeros((E,), dtype=jnp.float32)
        return {'x': x, 'W_in': W_in, 'b_in': b_in, 'W_g': W_g, 'b_g': b_g, 'W_out': W_out, 'b_out': b_out}
    _L0_attn_b_in = _L0_attn_b_setup()

    def _L0_ffn_setup():
        import jax, jax.numpy as jnp
        import numpy as np
        E = 16
        K = 4
        G = 4
        TG = 2
        NS = 2
        H = 128
        I = 176
        SCALE = 1.0

        def _gate(x2d, gate_w, gate_bias):
            T = x2d.shape[0]
            logits = x2d.astype(jnp.float32) @ gate_w.astype(jnp.float32).T
            scores = jax.nn.sigmoid(logits)
            sfc = scores + gate_bias[None, :]
            grp = sfc.reshape(T, G, E // G)
            top2, _ = jax.lax.top_k(grp, 2)
            group_scores = top2.sum(-1)
            _, gidx = jax.lax.top_k(group_scores, TG)
            gmask = jnp.zeros((T, G), sfc.dtype).at[jnp.arange(T)[:, None], gidx].set(1.0)
            smask = jnp.repeat(gmask, E // G, axis=1) > 0
            tmp = jnp.where(smask, sfc, 0.0)
            _, topk_idx = jax.lax.top_k(tmp, K)
            topk_w = jnp.take_along_axis(scores, topk_idx, axis=1)
            topk_w = topk_w / (topk_w.sum(-1, keepdims=True) + 1e-20)
            return (topk_idx, topk_w * SCALE)
        key = jax.random.key(seed)
        ks = jax.random.split(key, 8)
        bound = 1.0 / np.sqrt(H)
        return {'hidden_states': jax.random.normal(ks[0], (1, 128, H), jnp.float32), 'gate_w': jax.random.uniform(ks[1], (E, H), jnp.float32, -bound, bound), 'gate_bias': jnp.zeros((E,), jnp.float32), 'gate_proj': jax.random.normal(ks[2], (E, I, H), jnp.float32) * 0.02, 'up_proj': jax.random.normal(ks[3], (E, I, H), jnp.float32) * 0.02, 'down_proj': jax.random.normal(ks[4], (E, H, I), jnp.float32) * 0.02, 'shared_gate_w': jax.random.normal(ks[5], (I * NS, H), jnp.float32) * 0.02, 'shared_up_w': jax.random.normal(ks[6], (I * NS, H), jnp.float32) * 0.02, 'shared_down_w': jax.random.normal(ks[7], (H, I * NS), jnp.float32) * 0.02}
    _L0_ffn_in = _L0_ffn_setup()
    _d = {'L0_attn_a_x': _L0_attn_a_in['x'], 'L0_attn_a_Wq': _L0_attn_a_in['Wq'], 'L0_attn_a_Wk': _L0_attn_a_in['Wk'], 'L0_attn_a_Wv': _L0_attn_a_in['Wv'], 'L0_attn_a_Wo': _L0_attn_a_in['Wo'], 'L0_attn_b_W_in': _L0_attn_b_in['W_in'], 'L0_attn_b_b_in': _L0_attn_b_in['b_in'], 'L0_attn_b_W_g': _L0_attn_b_in['W_g'], 'L0_attn_b_b_g': _L0_attn_b_in['b_g'], 'L0_attn_b_W_out': _L0_attn_b_in['W_out'], 'L0_attn_b_b_out': _L0_attn_b_in['b_out'], 'L0_ffn_gate_w': _L0_ffn_in['gate_w'], 'L0_ffn_gate_bias': _L0_ffn_in['gate_bias'], 'L0_ffn_gate_proj': _L0_ffn_in['gate_proj'], 'L0_ffn_up_proj': _L0_ffn_in['up_proj'], 'L0_ffn_down_proj': _L0_ffn_in['down_proj'], 'L0_ffn_shared_gate_w': _L0_ffn_in['shared_gate_w'], 'L0_ffn_shared_up_w': _L0_ffn_in['shared_up_w'], 'L0_ffn_shared_down_w': _L0_ffn_in['shared_down_w']}
    _x0 = _d['L0_attn_a_x']
    _d['L0_attn_a_x'] = jax.random.normal(jax.random.fold_in(jax.random.key(seed), 1), (2, 1024, 128), dtype=_x0.dtype)
    del _x0
    return _d

def reference(L0_attn_a_x, L0_attn_a_Wq, L0_attn_a_Wk, L0_attn_a_Wv, L0_attn_a_Wo, L0_attn_b_W_in, L0_attn_b_b_in, L0_attn_b_W_g, L0_attn_b_b_g, L0_attn_b_W_out, L0_attn_b_b_out, L0_ffn_gate_w, L0_ffn_gate_bias, L0_ffn_gate_proj, L0_ffn_up_proj, L0_ffn_down_proj, L0_ffn_shared_gate_w, L0_ffn_shared_up_w, L0_ffn_shared_down_w):

    def _L0_attn_a_ref(x, Wq, Wk, Wv, Wo):
        import jax, jax.numpy as jnp
        import numpy as np
        D_MODEL = 128
        N_HEADS = 16
        HEAD_DIM = D_MODEL // N_HEADS
        ROPE_THETA = 10000.0
        EPS = 1e-06
        PAD_VAL = 1.0

        def _rope(x, cos, sin):
            x1 = x[..., 0::2]
            x2 = x[..., 1::2]
            r1 = x1 * cos - x2 * sin
            r2 = x1 * sin + x2 * cos
            return jnp.stack([r1, r2], axis=-1).reshape(x.shape)
        B, S, D = x.shape

        def split_heads(t):
            return t.reshape(B, S, N_HEADS, HEAD_DIM).transpose(0, 2, 1, 3)
        q = split_heads(x @ Wq)
        k = split_heads(x @ Wk)
        v = split_heads(x @ Wv)
        freqs = 1.0 / ROPE_THETA ** (jnp.arange(0, HEAD_DIM, 2, dtype=jnp.float32) / HEAD_DIM)
        ang = jnp.arange(S, dtype=jnp.float32)[:, None] * freqs[None, :]
        cos = jnp.cos(ang)[None, None]
        sin = jnp.sin(ang)[None, None]
        q = _rope(q, cos, sin)
        k = _rope(k, cos, sin)
        q = jax.nn.relu(q)
        k = jax.nn.relu(k)
        v_pad = jnp.pad(v, ((0, 0), (0, 0), (0, 0), (0, 1)), constant_values=PAD_VAL)
        vk = jnp.einsum('bhke,bhkd->bhed', v_pad, k)
        num = jnp.einsum('bhed,bhld->bhle', vk, q)
        attn = num[..., :-1] / (num[..., -1:] + EPS)
        out = attn.transpose(0, 2, 1, 3).reshape(B, S, D)
        return out @ Wo

    def _L0_attn_b_ref(x, W_in, b_in, W_g, b_g, W_out, b_out):
        import jax, jax.numpy as jnp
        import numpy as np
        from jax import lax
        B, S, E, SD = (8, 512, 128, 8)

        def _reference_tuple_inner(x, W_in, b_in, W_g, b_g, W_out, b_out):
            embed_dim = W_in.shape[0]
            combined = jnp.einsum('bse,ec->bsc', x, W_in) + b_in
            embed = combined[..., :embed_dim]
            state_in = combined[..., embed_dim:]
            gate = jax.nn.sigmoid(jnp.einsum('bsc,cd->bsd', combined, W_g) + b_g)

            def step(state, gs):
                g, si = gs
                new = g * state + (1.0 - g) * si
                return (new, new)
            state0 = jnp.zeros((x.shape[0], state_in.shape[-1]), dtype=x.dtype)
            g_t = jnp.moveaxis(gate, 1, 0)
            si_t = jnp.moveaxis(state_in, 1, 0)
            final_state, states = lax.scan(step, state0, (g_t, si_t))
            states = jnp.moveaxis(states, 0, 1)
            out = jnp.einsum('bsc,cd->bsd', jnp.concatenate([embed, states], axis=-1), W_out) + b_out
            return (out, final_state)
        return _reference_tuple_inner(x, W_in, b_in, W_g, b_g, W_out, b_out)[0]

    def _L0_ffn_ref(hidden_states, gate_w, gate_bias, gate_proj, up_proj, down_proj, shared_gate_w, shared_up_w, shared_down_w):
        import jax, jax.numpy as jnp
        import numpy as np
        E = 16
        K = 4
        G = 4
        TG = 2
        NS = 2
        H = 128
        I = 176
        SCALE = 1.0

        def _gate(x2d, gate_w, gate_bias):
            T = x2d.shape[0]
            logits = x2d.astype(jnp.float32) @ gate_w.astype(jnp.float32).T
            scores = jax.nn.sigmoid(logits)
            sfc = scores + gate_bias[None, :]
            grp = sfc.reshape(T, G, E // G)
            top2, _ = jax.lax.top_k(grp, 2)
            group_scores = top2.sum(-1)
            _, gidx = jax.lax.top_k(group_scores, TG)
            gmask = jnp.zeros((T, G), sfc.dtype).at[jnp.arange(T)[:, None], gidx].set(1.0)
            smask = jnp.repeat(gmask, E // G, axis=1) > 0
            tmp = jnp.where(smask, sfc, 0.0)
            _, topk_idx = jax.lax.top_k(tmp, K)
            topk_w = jnp.take_along_axis(scores, topk_idx, axis=1)
            topk_w = topk_w / (topk_w.sum(-1, keepdims=True) + 1e-20)
            return (topk_idx, topk_w * SCALE)
        orig_shape = hidden_states.shape
        x = hidden_states.reshape(-1, H)
        topk_idx, topk_w = _gate(x, gate_w, gate_bias)
        combine_w = (jax.nn.one_hot(topk_idx, E, dtype=x.dtype) * topk_w[..., None]).sum(1)
        g = jnp.einsum('th,eih->tei', x, gate_proj)
        u = jnp.einsum('th,eih->tei', x, up_proj)
        act = jax.nn.silu(g) * u
        y = jnp.einsum('tei,ehi,te->th', act, down_proj, combine_w)
        sg = x @ shared_gate_w.T
        su = x @ shared_up_w.T
        y = y + jax.nn.silu(sg) * su @ shared_down_w.T
        return y.reshape(orig_shape)
    x = L0_attn_a_x
    x = x + _L0_attn_a_ref(_layernorm(x, axis=-1), L0_attn_a_Wq, L0_attn_a_Wk, L0_attn_a_Wv, L0_attn_a_Wo)
    x = x + _L0_ffn_ref(_layernorm(x, axis=-1), L0_ffn_gate_w, L0_ffn_gate_bias, L0_ffn_gate_proj, L0_ffn_up_proj, L0_ffn_down_proj, L0_ffn_shared_gate_w, L0_ffn_shared_up_w, L0_ffn_shared_down_w)
    x = x + _L0_attn_b_ref(_layernorm(x, axis=-1), L0_attn_b_W_in, L0_attn_b_b_in, L0_attn_b_W_g, L0_attn_b_b_g, L0_attn_b_W_out, L0_attn_b_b_out)
    x = x + _L0_ffn_ref(_layernorm(x, axis=-1), L0_ffn_gate_w, L0_ffn_gate_bias, L0_ffn_gate_proj, L0_ffn_up_proj, L0_ffn_down_proj, L0_ffn_shared_gate_w, L0_ffn_shared_up_w, L0_ffn_shared_down_w)
    return x

_drawn_inputs = setup_inputs


def setup_inputs(seed=0):
    import zlib

    import numpy as np

    out = dict(_drawn_inputs(seed))
    spreads = {'L0_attn_b_b_in': (0.0, 0.1),
     'L0_attn_b_b_g': (0.0, 0.8),
     'L0_attn_b_b_out': (0.0, 0.1),
     'L0_ffn_gate_bias': (0.0, 0.8)}
    factors = {'L0_ffn_gate_w': 8.0,
     'L0_ffn_gate_proj': 8.0,
     'L0_ffn_up_proj': 8.0,
     'L0_ffn_down_proj': 8.0,
     'L0_ffn_shared_gate_w': 4.155,
     'L0_ffn_shared_up_w': 4.111,
     'L0_ffn_shared_down_w': 4.161}
    for name, (base, spread) in spreads.items():
        noise = np.random.default_rng([zlib.crc32(name.encode()), seed]).standard_normal(out[name].shape)
        drawn = base * np.exp(spread * noise) if base else spread * noise
        out[name] = jnp.asarray(drawn.astype(out[name].dtype))
    for name, factor in factors.items():
        out[name] = (out[name] * factor).astype(out[name].dtype)
    return out
```

```python
import concourse.bass as bass
from concourse import mybir
from contextlib import ExitStack

P = 128
BATCH, SEQ, D = 2, 1024, 128
TILES = BATCH * SEQ // P
BT = 4
BLK = BT * P
NBLK = TILES // BT
HEADS, HD = 16, 8
E, I, NS = 16, 176, 2
GROUPS, TOPG, TOPK = 4, 2, 4
GE = E // GROUPS
EU = E * I // P
SHARED = I * NS
UNITS = EU + -(-SHARED // P)
HID = UNITS * P
SD = 8
KVW = D + HEADS
LN_EPS, DEN_EPS, TOPK_EPS = 1e-5, 1e-6, 1e-20
PARTS = 3
WCH = 5
PIECES = UNITS // WCH
RING = 4

Y_OUT, Y_TURN, LN1, LN1_POW, LN1_Z, Z1_TURN, Z1_OUT = 1, 2, 3, 4, 5, 6, 7
EMB, EMB_OUT, GATE, GATE_SIG, SCAN, MIX = 8, 9, 10, 11, 12, 14
LN2, LN2_POW, LN2_Z, Z2_TURN, Z2_OUT, LOGIT, SCORE, ROUTE, CW_TURN = 15, 16, 17, 18, 19, 20, 21, 22, 24


def hybrid_kernel(nc, A, out):
    f32, f32r, bf16 = mybir.dt.float32, mybir.dt.float32r, mybir.dt.bfloat16
    ALU, ACT, AX = mybir.AluOpType, mybir.ActivationFunctionType, mybir.AxisListType
    ds = bass.ds
    ctx = ExitStack()
    with ctx:
        def sb(name, shape, dt=f32):
            return ctx.enter_context(nc.sbuf_tensor(name, shape, dt))

        def sem(name):
            return ctx.enter_context(nc.semaphore(name))

        W_hi = [sb(f"{n}_hi", [P, HID], f32r) for n in ("gate_proj", "up_proj", "down_proj")]
        W_lo = [sb(f"{n}_lo", [P, HID], f32r) for n in ("gate_proj", "up_proj", "down_proj")]
        stage = sb("stage", [P, RING, WCH * P])
        xh = sb("xh", [P, NBLK * BLK], f32r)
        xl = sb("xl", [P, NBLK * BLK], f32r)
        cwT = sb("cwT", [P, NBLK * BLK], bf16)
        expert_of = sb("expert_of", [P, EU * P], bf16)
        x_tok = sb("x_tok", [P, TILES, D])
        silu_sb = sb("silu_sb", [P, 2, BLK])
        act_sb = sb("act_sb", [P, 2, BLK])
        hid_sb = sb("hid_sb", [P, 2, BLK])
        hid_hi = sb("hid_hi", [P, 5, BLK], f32r)
        hid_lo = sb("hid_lo", [P, 5, BLK], f32r)
        w_qkv = sb("w_qkv", [P, 3 * D])
        w_o = sb("w_o", [P, D])
        cos_t = sb("cos_t", [P, SEQ // P, D // 2])
        sin_t = sb("sin_t", [P, SEQ // P, 2, D // 2])
        head_mask = sb("head_mask", [P, KVW])
        rot_a = sb("rot_a", [P, 2, 2, 2, D // 2])
        rot_b = sb("rot_b", [P, 2, 2, 2, D // 2])
        rot = sb("rot", [P, 2, 2, 2, D // 2])
        qk = sb("qk", [P, BT, 2, D])
        v_pad = sb("v_pad", [P, BT, KVW])
        qT = sb("qT", [P, 2 * BLK])
        kv_half = sb("kv_half", [P, KVW])
        kv_sum = sb("kv_sum", [P, KVW])
        kv = sb("kv", [P, KVW])
        den = sb("den", [P, BT * HEADS])
        rden = sb("rden", [P, BT * HEADS])
        xcur = sb("xcur", [P, BT, D])
        z = sb("z", [P, BT, D])
        zT = sb("zT", [P, BLK])
        stats = sb("stats", [P, BT, 6])
        mv = sb("mv", [P, 5, BT])
        mean = sb("mean", [P, BT])
        vpe = sb("vpe", [P, BT])
        rstd = sb("rstd", [P, BT])
        neg_half = sb("neg_half", [P, BT])
        w_in = sb("w_in", [P, D + SD])
        b_in = sb("b_in", [P, 1])
        b_in_s = sb("b_in_s", [SD, 1])
        w_g = sb("w_g", [P, SD])
        w_g_s = sb("w_g_s", [SD, SD])
        b_g = sb("b_g", [SD, 1])
        w_out = sb("w_out", [P, D])
        w_out_s = sb("w_out_s", [SD + 1, D])
        embT = sb("embT", [P, BLK])
        siT = sb("siT", [SD, BLK])
        gT = sb("gT", [SD, BLK])
        omgT = sb("omgT", [SD, BLK])
        inT = sb("inT", [SD, BLK])
        stT = sb("stT", [SD + 1, BLK])
        carry = sb("carry", [SD, 1])
        keep = sb("keep", [SD, NBLK])
        w_route = sb("w_route", [P, E])
        bias_route = sb("bias_route", [P, E])
        lower_e = sb("lower_e", [P, E, E], bf16)
        lower_g = sb("lower_g", [P, GROUPS, GROUPS])
        thr_e = sb("thr_e", [P, E])
        thr_g = sb("thr_g", [P, GROUPS])
        scores = sb("scores", [P, BT, E])
        sfc = sb("sfc", [P, BT, E])
        pair_hi = sb("pair_hi", [P, BT * E // 2])
        pair_lo = sb("pair_lo", [P, BT * E // 2])
        quad = sb("quad", [P, 5, BT * GROUPS])
        beats_g = sb("beats_g", [P, BT, GROUPS, GROUPS])
        rank_g = sb("rank_g", [P, 4, BT * GROUPS])
        masked = sb("masked", [P, BT, E])
        beats_e = sb("beats_e", [P, BT, E, E], bf16)
        rank_e = sb("rank_e", [P, 4, BT * E])
        wsum = sb("wsum", [P, 3, BT])
        cw = sb("cw", [P, BT, E])
        cw_left = sb("cw_left", [P, 2, BT, E])
        cw_parts = sb("cw_parts", [P, BT, P], bf16)
        ident = sb("ident", [P, P])
        ident_bf = sb("ident_bf", [P, P], bf16)

        ps = ctx.enter_context(nc.psum_tensor("ps", [P, 8, BLK], f32))
        PS_G, PS_U, PS_C, PS_Y, PS_A, PS_B = (0, 1), (2, 3), 4, 5, 6, 7

        def bank(b):
            return ps[:, b, :]

        def tiles(b):
            return ps[:, b, :].rearrange("p (t d) -> p t d", t=BT)

        psB_bf = ps[:, PS_B, 0:BLK // 2].bitcast(bf16)

        x_loaded, attn_loaded, const_loaded = sem("x_loaded"), sem("attn_loaded"), sem("const_loaded")
        piece_loaded = [sem(f"piece_loaded{i}") for i in range(RING)]
        piece_hi, piece_lo = sem("piece_hi"), sem("piece_lo")
        ident_zero, ident_ready = sem("ident_zero"), sem("ident_ready")
        stats_ready, mv_ready, vpe_ready = sem("stats_ready"), sem("mv_ready"), sem("vpe_ready")
        rstd_ready, z_ready, z_turned, zT_ready = sem("rstd_ready"), sem("z_ready"), sem("z_turned"), sem("zT_ready")
        xcur_ready = sem("xcur_ready")
        qkv_ready, rot_mul, rot_ready = sem("qkv_ready"), sem("rot_mul"), sem("rot_ready")
        v_ready, qk_ready, kv_turned = sem("v_ready"), sem("qk_ready"), sem("kv_turned")
        kv_summed = sem("kv_summed")
        num_ready, den_ready, rden_ready, att_ready = sem("num_ready"), sem("den_ready"), sem("rden_ready"), sem("att_ready")
        att_turned, attT_ready, proj_ready = sem("att_turned"), sem("attT_ready"), sem("proj_ready")
        logits_ready, scores_ready, route_step = sem("logits_ready"), sem("scores_ready"), sem("route_step")
        cw_split = sem("cw_split")
        cw_turned, routed, xh_ready, xl_ready = sem("cw_turned"), sem("routed"), sem("xh_ready"), sem("xl_ready")
        stage_done = sem("stage_done")
        g_ready, u_ready, c_ready = sem("g_ready"), sem("u_ready"), sem("c_ready")
        silu_ready, act_ready, hid_ready = sem("silu_ready"), sem("act_ready"), sem("hid_ready")
        hi_ready, lo_ready, down_done, y_out = sem("hi_ready"), sem("lo_ready"), sem("down_done"), sem("y_out")
        y_turned, emb_ps, embT_ready, siT_ready = sem("y_turned"), sem("emb_ps"), sem("embT_ready"), sem("siT_ready")
        gate_ps, gT_ready, scan_step, mix_ready = sem("gate_ps"), sem("gT_ready"), sem("scan_step"), sem("mix_ready")
        out_turned, out_ready, out_stored = sem("out_turned"), sem("out_ready"), sem("out_stored")

        block = ctx.enter_context(nc.Block())

        N_ATTN, N_CONST = 5, 17
        ROUTE_STEPS, CW_SPLITS, MV_STEPS = 26, 2 * PARTS - 1, 6
        PER_BATCH = 4

        def beside(side, u):
            while side is not None and side[1] <= u:
                side[1] = next(side[0], UNITS + 1)

        def started(side):
            return [side, next(side, UNITS + 1)]

        def finish(side):
            for _ in side:
                pass

        def freed(p, u):
            return p * UNITS + u - 1 if u >= 2 else p * UNITS - u

        @block.sync
        def _(sp):
            sp.dma_start(x_tok[:, :, :], A["x"].rearrange("(t p) d -> p t d", p=P)).then_inc(x_loaded, 16)
            for dst, src in ((w_qkv, "w_qkv"), (w_o, "w_o"), (head_mask, "head_mask")):
                sp.dma_start(dst[:, :], A[src]).then_inc(attn_loaded, 16)
            sp.dma_start(cos_t[:, :, :], A["cos"]).then_inc(attn_loaded, 16)
            sp.dma_start(sin_t[:, :, :, :], A["sin"]).then_inc(attn_loaded, 16)
            for dst, src in ((w_route, "w_route"), (bias_route, "bias_route"), (thr_e, "thr_e"), (thr_g, "thr_g"),
                             (b_in, "b_in"), (b_in_s, "b_in_s"), (w_g, "w_g"), (w_g_s, "w_g_s"), (b_g, "b_g"),
                             (w_out, "w_out"), (w_out_s, "w_out_s"), (keep, "keep"), (w_in, "w_in"),
                             (neg_half, "neg_half")):
                sp.dma_start(dst[:, :], A[src]).then_inc(const_loaded, 16)
            sp.dma_start(lower_e[:, :, :], A["lower_e"]).then_inc(const_loaded, 16)
            sp.dma_start(lower_g[:, :, :], A["lower_g"]).then_inc(const_loaded, 16)
            sp.dma_start(expert_of[:, :], A["expert_of"]).then_inc(const_loaded, 16)
            for n in range(3 * PIECES):
                if n >= RING:
                    sp.wait_ge(piece_lo, n - RING + 1)
                w, c = n // PIECES, n % PIECES
                sp.dma_start(stage[:, n % RING, :], A[("gate_proj", "up_proj", "down_proj")[w]]
                             [:, c * WCH * P:(c + 1) * WCH * P]).then_inc(piece_loaded[n % RING], 16)
            def store(o):
                sp.wait_ge(out_ready, o + 1)
                sp.dma_start(out.rearrange("(b t p) d -> b p t d", p=P, t=BT)[o], xcur[:, :, :]).then_inc(out_stored, 16)
            for o in range(NBLK):
                store(o)
            sp.wait_ge(out_stored, 16 * NBLK)

        @block.gpsimd
        def _(pool):
            nc.gpsimd.memset(ident[:, :], 0.0).then_inc(ident_zero, 1)
            nc.gpsimd.memset(v_pad[:, :, :], 1.0)
            nc.gpsimd.memset(cw_parts[:, :, :], 0.0)
            nc.gpsimd.memset(stT[:, :], 1.0)
            nc.gpsimd.memset(carry[:, :], 0.0)
            pool.wait_ge(ident_zero, 1)
            nc.gpsimd.affine_select(out=ident[:, :], in_=ident[:, :], compare_op=ALU.not_equal, fill=1.0,
                                    base=0, pattern=[[-1, P]], channel_multiplier=1).then_inc(ident_ready, 1)
            pool.wait_ge(ident_ready, 1)
            nc.gpsimd.tensor_copy(ident_bf[:, :], ident[:, :]).then_inc(ident_ready, 1)

            def ln(k):
                pool.wait_ge(vpe_ready, k + 1)
                nc.gpsimd.tensor_tensor(rstd[:, :], vpe[:, :], neg_half[:, :], ALU.pow).then_inc(rstd_ready, 1)

            def keep_x(n, b):
                pool.wait_ge(xcur_ready, n + 1)
                nc.gpsimd.tensor_copy(x_tok[:, ds(b * BT, BT), :], xcur[:, :, :])

            def split_x(r, slot):
                pool.wait_ge(xh_ready, r + 1)
                nc.gpsimd.tensor_tensor(xl[:, ds(slot * BLK, BLK)], zT[:, :],
                                        xh[:, ds(slot * BLK, BLK)].bitcast(f32), ALU.subtract).then_inc(xl_ready, 1)

            def attn_a(k, a):
                ln(k)
                for t in range(BT):
                    n = a * BT + t
                    pool.wait_ge(rot_mul, 2 * n + 2)
                    if t >= 2:
                        pool.wait_ge(qk_ready, n - 1)
                    nc.gpsimd.tensor_tensor(rot[:, t % 2, :, 0, :], rot_a[:, t % 2, :, 0, :],
                                            rot_b[:, t % 2, :, 1, :], ALU.add)
                    nc.gpsimd.tensor_tensor(rot[:, t % 2, :, 1, :], rot_a[:, t % 2, :, 1, :],
                                            rot_b[:, t % 2, :, 0, :], ALU.add).then_inc(rot_ready, 1)

            def split_lo(n):
                w, c = n // PIECES, n % PIECES
                cols = slice(c * WCH * P, (c + 1) * WCH * P)
                pool.wait_ge(piece_hi, n + 1)
                nc.gpsimd.tensor_tensor(W_lo[w][:, cols], stage[:, n % RING, :], W_hi[w][:, cols].bitcast(f32), ALU.subtract).then_inc(piece_lo, 1)

            def pre(i):
                for a0 in range(2):
                    attn_a(i * 4 + a0, i * 2 + a0)
                for a0 in range(2):
                    keep_x(i * 2 + a0, i * 2 + a0)
                    ln(i * 4 + 2 + a0)
                    split_x(i * 2 + a0, i * 2 + a0)

            pool.wait_ge(const_loaded, 16 * N_CONST)
            with pool.Fori(0, BATCH) as i:
                pre(i)
            for n in range(3 * PIECES):
                split_lo(n)

            def mid(m):
                yield LN1_POW
                ln(8 + 2 * m)
                yield LN2
                keep_x(4 + 2 * m + 1, m)
                yield LN2_POW
                ln(8 + 2 * m + 1)
                yield Z2_OUT
                split_x(NBLK + m, m)

            def ffn(p, side=None):
                for u in range(UNITS):
                    pool.wait_ge(hi_ready, p * UNITS + u + 1)
                    nc.gpsimd.tensor_tensor(hid_lo[:, u % 5, :], hid_sb[:, u % 2, :],
                                            hid_hi[:, u % 5, :].bitcast(f32), ALU.subtract).then_inc(lo_ready, 1)
                    beside(side, u)
                beside(side, UNITS)

            ffn(0)
            with pool.Fori(1, NBLK + 1) as p:
                ffn(p, started(mid(p - 1)))
            with pool.Fori(NBLK + 1, 2 * NBLK) as p:
                ffn(p)

        @block.scalar
        def _(act):
            def zT_copy(k):
                act.wait_ge(z_turned, k + 1)
                nc.scalar.activation(zT[:, :], bank(PS_B), ACT.Copy).then_inc(zT_ready, 1)

            def attn_a(k, a, a0):
                zT_copy(k)
                for t in range(BT):
                    n = a * BT + t
                    src = bank((PS_A, PS_B)[t % 2])
                    act.wait_ge(rot_mul, 2 * n + 2)
                    nc.scalar.activation(v_pad[:, t, 0:D], src[:, 2 * D:3 * D], ACT.Copy).then_inc(v_ready, 1)
                    act.wait_ge(rot_ready, n + 1)
                    nc.scalar.activation(qk[:, t, :, :], rot[:, t % 2, :, :, :].rearrange("p a b d -> p a (b d)"),
                                         ACT.Relu).then_inc(qk_ready, 1)
                act.wait_ge(kv_turned, a + 1)
                nc.scalar.activation(qT[:, a0 * BLK:(a0 + 1) * BLK], bank(PS_A), ACT.Copy).then_inc(stage_done, 1)

            def route(k, r, slot):
                act.wait_ge(z_turned, k + 1)
                nc.scalar.activation(zT[:, :], bank(PS_B), ACT.Copy).then_inc(zT_ready, 1)
                nc.scalar.activation(xh[:, ds(slot * BLK, BLK)], bank(PS_B), ACT.Copy).then_inc(xh_ready, 1)
                yield SCORE
                act.wait_ge(logits_ready, r + 1)
                nc.scalar.activation(scores[:, :, :].rearrange("p t e -> p (t e)"), ps[:, PS_A, 0:BT * E],
                                     ACT.Sigmoid).then_inc(scores_ready, 1)
                yield CW_TURN
                act.wait_ge(cw_turned, r + 1)
                act.wait_ge(xl_ready, r + 1)
                nc.scalar.activation(cwT[:, ds(slot * BLK, BLK)], psB_bf,
                                     ACT.Copy).then_inc(routed, 1)

            def attn_b(k, b):
                act.wait_ge(att_turned, b + 1)
                nc.scalar.activation(zT[:, :], bank(PS_B), ACT.Copy).then_inc(attT_ready, 1)
                finish(route(k, b, b))

            def split_hi(n):
                w, c = n // PIECES, n % PIECES
                act.wait_ge(piece_loaded[n % RING], 16 * (n // RING + 1))
                nc.scalar.activation(W_hi[w][:, c * WCH * P:(c + 1) * WCH * P], stage[:, n % RING, :],
                                     ACT.Copy).then_inc(piece_hi, 1)

            def pre(i):
                for a0 in range(2):
                    attn_a(i * 4 + a0, i * 2 + a0, a0)
                for a0 in range(2):
                    attn_b(i * 4 + 2 + a0, i * 2 + a0)

            act.wait_ge(ident_ready, 2)
            with act.Fori(0, BATCH) as i:
                pre(i)
            for n in range(3 * PIECES):
                split_hi(n)

            def y_copy(p):
                act.wait_ge(down_done, p * UNITS)
                nc.scalar.activation(zT[:, :], bank(PS_Y), ACT.Copy).then_inc(y_out, 1)

            def mid(m):
                yield Y_OUT
                y_copy(m + 1)
                yield Z1_OUT
                zT_copy(8 + 2 * m)
                yield EMB_OUT
                act.wait_ge(emb_ps, m + 1)
                nc.scalar.activation(embT[:, :], bank(PS_A), ACT.Identity, bias=b_in[:, 0:1]).then_inc(embT_ready, 1)
                yield GATE_SIG
                act.wait_ge(gate_ps, m + 1)
                nc.scalar.activation(gT[:, :], ps[0:SD, PS_A, :], ACT.Sigmoid, bias=b_g[:, 0:1]).then_inc(gT_ready, 1)
                yield Z2_OUT
                yield from route(8 + 2 * m + 1, NBLK + m, m)

            def last(o):
                yield Y_OUT
                y_copy(NBLK + 1 + o)

            def ffn(p, first=False, side=None):
                def hi(u):
                    act.wait_ge(hid_ready, p * UNITS + u + 1)
                    if not first or u >= 5:
                        act.wait_ge(down_done, p * UNITS + u - 4)
                    nc.scalar.activation(hid_hi[:, u % 5, :], hid_sb[:, u % 2, :], ACT.Copy).then_inc(hi_ready, 1)
                for u in range(UNITS):
                    act.wait_ge(g_ready, p * UNITS + u + 1)
                    if not first or u >= 2:
                        act.wait_ge(hid_ready if u >= EU + 2 or u < 2 else act_ready,
                                    freed_s(p, u))
                    nc.scalar.activation(silu_sb[:, u % 2, :], bank(PS_G[u % 2]), ACT.Silu).then_inc(silu_ready, 1)
                    if u >= 1:
                        hi(u - 1)
                    beside(side, u)
                hi(UNITS - 1)
                beside(side, UNITS)

            def freed_s(p, u):
                if u < 2:
                    return p * UNITS - u
                if u >= EU + 2:
                    return p * UNITS + u - 1
                return p * EU + u - 1

            act.wait_ge(const_loaded, 16 * N_CONST)
            ffn(0, first=True)
            with act.Fori(1, NBLK + 1) as p:
                ffn(p, side=started(mid(p - 1)))
            with act.Fori(NBLK + 1, 2 * NBLK) as p:
                ffn(p, side=started(last(p - NBLK - 1)))
            finish(last(NBLK - 1))

        @block.vector
        def _(dve):
            def ln(k, src):
                for t in range(BT):
                    nc.vector.bn_stats(stats[:, t, :], src(t)).then_inc(stats_ready, 1)
                dve.wait_ge(stats_ready, BT * k + BT)
                nc.vector.tensor_tensor(mv[:, 0, :], stats[:, :, 1], stats[:, :, 4], ALU.add).then_inc(mv_ready, 1)
                nc.vector.tensor_tensor(mv[:, 1, :], stats[:, :, 1], stats[:, :, 4], ALU.subtract).then_inc(mv_ready, 1)
                nc.vector.tensor_tensor(mv[:, 2, :], stats[:, :, 2], stats[:, :, 5], ALU.add).then_inc(mv_ready, 1)
                dve.wait_ge(mv_ready, MV_STEPS * k + 3)
                nc.vector.scalar_tensor_tensor(out=mv[:, 3, :], in0=mv[:, 1, :], scalar=0.25, in1=mv[:, 1, :],
                                               op0=ALU.mult, op1=ALU.mult).then_inc(mv_ready, 1)
                nc.vector.tensor_scalar(mv[:, 4, :], mv[:, 2, :], 1.0 / D, LN_EPS, ALU.mult, ALU.add).then_inc(mv_ready, 1)
                nc.vector.tensor_scalar(mean[:, :], mv[:, 0, :], 0.5, None, ALU.mult).then_inc(mv_ready, 1)
                dve.wait_ge(mv_ready, MV_STEPS * k + 6)
                nc.vector.tensor_tensor(vpe[:, :], mv[:, 3, :], mv[:, 4, :], ALU.add).then_inc(vpe_ready, 1)

            def ln_z(k, src):
                dve.wait_ge(rstd_ready, k + 1)
                for t in range(BT):
                    nc.vector.tensor_scalar(z[:, t, :], src(t), mean[:, t:t + 1], rstd[:, t:t + 1],
                                            ALU.subtract, ALU.mult).then_inc(z_ready, 1)

            def cur(t):
                return xcur[:, t, :]

            def attn_a(k, a, a0, i):
                def src(t):
                    return x_tok[:, ds(a * BT + t, 1), :].rearrange("p t d -> p (t d)")
                ln(k, src)
                ln_z(k, src)
                for t in range(BT):
                    n = a * BT + t
                    pst = ps[:, (PS_A, PS_B)[t % 2], 0:2 * D].rearrange("p (a b d) -> p a b d", a=2, b=2)
                    dve.wait_ge(qkv_ready, n + 1)
                    if t >= 2:
                        dve.wait_ge(rot_ready, n - 1)
                    nc.vector.tensor_tensor(
                        rot_a[:, t % 2].rearrange("p a b d -> p (a b) d"), pst.rearrange("p a b d -> p (a b) d"),
                        cos_t[:, a0 * BT + t:a0 * BT + t + 1, :].to_broadcast([P, 4, D // 2]), ALU.mult).then_inc(rot_mul, 1)
                    nc.vector.tensor_tensor(
                        rot_b[:, t % 2], pst,
                        sin_t[:, a0 * BT + t:a0 * BT + t + 1, :, :].to_broadcast([P, 2, 2, D // 2]), ALU.mult).then_inc(rot_mul, 1)
                dve.wait_ge(kv_turned, a + 1)
                if a0 == 0:
                    nc.vector.tensor_copy(kv_half[:, :], ps[:, PS_B, 0:KVW]).then_inc(stage_done, 1)
                else:
                    nc.vector.tensor_tensor(kv_sum[:, :], ps[:, PS_B, 0:KVW], kv_half[:, :], ALU.add).then_inc(kv_summed, 1)
                    dve.wait_ge(kv_summed, i + 1)
                    nc.vector.tensor_tensor(kv[:, :], kv_sum[:, :], head_mask[:, :], ALU.mult).then_inc(stage_done, 1)

            def attn_b(k, b):
                dve.wait_ge(num_ready, b + 1)
                nc.vector.tensor_scalar(den[:, :], ps[:, PS_B, 0:BT * HEADS], DEN_EPS, None, ALU.add).then_inc(den_ready, 1)
                dve.wait_ge(den_ready, b + 1)
                nc.vector.reciprocal(rden[:, :], den[:, :]).then_inc(rden_ready, 1)
                dve.wait_ge(rden_ready, b + 1)
                nc.vector.tensor_tensor(z[:, :, :].rearrange("p t (h e) -> p (t h) e", h=HEADS),
                                        bank(PS_A).rearrange("p (h e) -> p h e", e=HD),
                                        rden[:, :, None].to_broadcast([P, BT * HEADS, HD]), ALU.mult).then_inc(att_ready, 1)
                dve.wait_ge(proj_ready, b + 1)
                nc.vector.tensor_tensor(xcur[:, :, :], tiles(PS_A), x_tok[:, ds(b * BT, BT), :], ALU.add).then_inc(xcur_ready, 1)
                dve.wait_ge(xcur_ready, b + 1)
                ln(k, cur)
                ln_z(k, cur)
                finish(route(b, b))

            def route(r, slot):
                yield ROUTE
                dve.wait_ge(scores_ready, r + 1)
                done = [0]

                def step(ins):
                    done[0] += 1
                    ins.then_inc(route_step, 1)

                def after(n):
                    dve.wait_ge(route_step, r * ROUTE_STEPS + n)

                def tt(o, a, b, op):
                    step(nc.vector.tensor_tensor(o, a, b, op))

                tt(sfc[:, :, :], scores[:, :, :], bias_route[:, None, :].to_broadcast([P, BT, E]), ALU.add)
                after(1)
                pairs = sfc[:, :, :].rearrange("p t (g two) -> p (t g) two", two=2)
                tt(pair_hi[:, :], pairs[:, :, 0], pairs[:, :, 1], ALU.max)
                tt(pair_lo[:, :], pairs[:, :, 0], pairs[:, :, 1], ALU.min)
                hi2 = pair_hi[:, :].rearrange("p (g two) -> p g two", two=2)
                lo2 = pair_lo[:, :].rearrange("p (g two) -> p g two", two=2)
                after(3)
                tt(quad[:, 0, :], hi2[:, :, 0], hi2[:, :, 1], ALU.max)
                tt(quad[:, 1, :], hi2[:, :, 0], hi2[:, :, 1], ALU.min)
                tt(quad[:, 2, :], lo2[:, :, 0], lo2[:, :, 1], ALU.max)
                after(6)
                tt(quad[:, 3, :], quad[:, 1, :], quad[:, 2, :], ALU.max)
                after(7)
                tt(quad[:, 4, :], quad[:, 0, :], quad[:, 3, :], ALU.add)
                after(8)
                gs = quad[:, 4, :].rearrange("p (t g) -> p t g", t=BT)
                tt(beats_g[:, :, :, :], gs[:, :, None, :].to_broadcast([P, BT, GROUPS, GROUPS]),
                   gs[:, :, :, None].to_broadcast([P, BT, GROUPS, GROUPS]), ALU.is_ge)
                after(9)
                tt(beats_g[:, :, :, :], beats_g[:, :, :, :],
                   lower_g[:, None, :, :].to_broadcast([P, BT, GROUPS, GROUPS]), ALU.mult)
                after(10)
                step(nc.vector.tensor_reduce(rank_g[:, 0, :], beats_g[:, :, :, :].rearrange("p t i j -> p (t i) j"),
                                             AX.X, ALU.add))
                step(nc.vector.tensor_reduce(rank_g[:, 1, :].rearrange("p (t i) -> p t i", t=BT),
                                             beats_g[:, :, :, :].rearrange("p t i j -> p t j i"), AX.X, ALU.add))
                after(12)
                tt(rank_g[:, 2, :], rank_g[:, 0, :], rank_g[:, 1, :], ALU.subtract)
                after(13)
                tt(rank_g[:, 3, :].rearrange("p (t g) -> p t g", t=BT), rank_g[:, 2, :].rearrange("p (t g) -> p t g", t=BT),
                   thr_g[:, None, :].to_broadcast([P, BT, GROUPS]), ALU.is_lt)
                after(14)
                tt(masked[:, :, :].rearrange("p t (g e) -> p (t g) e", e=GE),
                   sfc[:, :, :].rearrange("p t (g e) -> p (t g) e", e=GE),
                   rank_g[:, 3, :, None].to_broadcast([P, BT * GROUPS, GE]), ALU.mult)
                after(15)
                tt(beats_e[:, :, :, :], masked[:, :, None, :].to_broadcast([P, BT, E, E]),
                   masked[:, :, :, None].to_broadcast([P, BT, E, E]), ALU.is_ge)
                after(16)
                tt(beats_e[:, :, :, :], beats_e[:, :, :, :], lower_e[:, None, :, :].to_broadcast([P, BT, E, E]), ALU.mult)
                after(17)
                step(nc.vector.tensor_reduce(rank_e[:, 0, :], beats_e[:, :, :, :].rearrange("p t i j -> p (t i) j"),
                                             AX.X, ALU.add))
                step(nc.vector.tensor_reduce(rank_e[:, 1, :].rearrange("p (t i) -> p t i", t=BT),
                                             beats_e[:, :, :, :].rearrange("p t i j -> p t j i"), AX.X, ALU.add))
                after(19)
                tt(rank_e[:, 2, :], rank_e[:, 0, :], rank_e[:, 1, :], ALU.subtract)
                after(20)
                tt(rank_e[:, 3, :].rearrange("p (t g) -> p t g", t=BT), rank_e[:, 2, :].rearrange("p (t g) -> p t g", t=BT),
                   thr_e[:, None, :].to_broadcast([P, BT, E]), ALU.is_lt)
                after(21)
                tt(masked[:, :, :], scores[:, :, :], rank_e[:, 3, :].rearrange("p (t e) -> p t e", t=BT), ALU.mult)
                after(22)
                step(nc.vector.tensor_reduce(wsum[:, 0, :], masked[:, :, :], AX.X, ALU.add))
                after(23)
                step(nc.vector.tensor_scalar(wsum[:, 1, :], wsum[:, 0, :], TOPK_EPS, None, ALU.add))
                after(24)
                step(nc.vector.reciprocal(wsum[:, 2, :], wsum[:, 1, :]))
                after(25)
                tt(cw[:, :, :], masked[:, :, :], wsum[:, 2, :, None].to_broadcast([P, BT, E]), ALU.mult)
                after(26)
                left = cw[:, :, :]
                for part in range(PARTS):
                    here = cw_parts[:, :, part * E:(part + 1) * E]
                    nc.vector.tensor_copy(here, left).then_inc(cw_split, 1)
                    dve.wait_ge(cw_split, r * CW_SPLITS + 2 * part + 1)
                    if part < PARTS - 1:
                        nc.vector.tensor_tensor(cw_left[:, part, :, :], left, here, ALU.subtract).then_inc(cw_split, 1)
                        dve.wait_ge(cw_split, r * CW_SPLITS + 2 * part + 2)
                        left = cw_left[:, part, :, :]
                assert done[0] == ROUTE_STEPS

            def pre(i):
                for a0 in range(2):
                    if a0:
                        dve.wait_ge(stage_done, i * PER_BATCH + 2)
                    attn_a(i * 4 + a0, i * 2 + a0, a0, i)
                for a0 in range(2):
                    attn_b(i * 4 + 2 + a0, i * 2 + a0)

            dve.wait_ge(ident_ready, 2)
            dve.wait_ge(x_loaded, 16)
            dve.wait_ge(attn_loaded, 16 * N_ATTN)
            dve.wait_ge(const_loaded, 16 * N_CONST)
            with dve.Fori(0, BATCH) as i:
                pre(i)

            def mid(m):
                yield LN1
                dve.wait_ge(y_turned, m + 1)
                nc.vector.tensor_tensor(xcur[:, :, :], tiles(PS_A), x_tok[:, ds(m * BT, BT), :], ALU.add).then_inc(xcur_ready, 1)
                dve.wait_ge(xcur_ready, NBLK + 2 * m + 1)
                ln(8 + 2 * m, cur)
                yield LN1_Z
                ln_z(8 + 2 * m, cur)
                yield EMB_OUT
                dve.wait_ge(emb_ps, m + 1)
                nc.vector.tensor_scalar(siT[:, :], ps[0:SD, PS_B, :], b_in_s[:, 0:1], None, ALU.add).then_inc(siT_ready, 1)
                yield SCAN
                dve.wait_ge(gT_ready, m + 1)
                nc.vector.tensor_scalar(omgT[:, :], gT[:, :], -1.0, 1.0, ALU.mult, ALU.add).then_inc(scan_step, 1)
                dve.wait_ge(scan_step, 4 * m + 1)
                nc.vector.tensor_tensor(inT[:, :], omgT[:, :], siT[:, :], ALU.mult).then_inc(scan_step, 1)
                dve.wait_ge(scan_step, 4 * m + 2)
                nc.vector.tensor_tensor_scan(stT[0:SD, :], gT[:, :], inT[:, :], carry[:, 0:1], ALU.mult, ALU.add).then_inc(scan_step, 1)
                dve.wait_ge(scan_step, 4 * m + 3)
                nc.vector.tensor_tensor(carry[:, 0:1], stT[0:SD, BLK - 1:BLK], keep[:, ds(m, 1)], ALU.mult).then_inc(scan_step, 1)
                yield LN2
                dve.wait_ge(mix_ready, m + 1)
                nc.vector.tensor_tensor(xcur[:, :, :], tiles(PS_A), xcur[:, :, :], ALU.add).then_inc(xcur_ready, 1)
                dve.wait_ge(xcur_ready, NBLK + 2 * m + 2)
                ln(8 + 2 * m + 1, cur)
                yield LN2_Z
                ln_z(8 + 2 * m + 1, cur)
                yield Z2_OUT
                yield from route(NBLK + m, m)

            def last(o):
                yield LN1
                dve.wait_ge(out_turned, o + 1)
                nc.vector.tensor_tensor(xcur[:, :, :], tiles(PS_A), x_tok[:, ds(o * BT, BT), :], ALU.add).then_inc(out_ready, 1)
                yield ROUTE
                dve.wait_ge(out_stored, 16 * (o + 1))

            def ffn(p, first=False, side=None):
                for u in range(UNITS):
                    n = p * UNITS + u
                    routed_unit = u < EU
                    dve.wait_ge(silu_ready, n + 1)
                    dve.wait_ge(u_ready, n + 1)
                    dst, told = (act_sb, act_ready) if routed_unit else (hid_sb, hid_ready)
                    if not first or u >= 2:
                        if routed_unit:
                            dve.wait_ge(hid_ready, freed(p, u))
                        else:
                            dve.wait_ge(lo_ready, freed(p, u))
                    nc.vector.tensor_tensor(dst[:, u % 2, :], bank(PS_U[u % 2]), silu_sb[:, u % 2, :], ALU.mult).then_inc(told, 1)
                    if routed_unit:
                        dve.wait_ge(c_ready, p * EU + u + 1)
                        dve.wait_ge(act_ready, p * EU + u + 1)
                        if not first or u >= 2:
                            dve.wait_ge(lo_ready, freed(p, u))
                        nc.vector.tensor_tensor(hid_sb[:, u % 2, :], bank(PS_C), act_sb[:, u % 2, :], ALU.mult).then_inc(hid_ready, 1)
                    beside(side, u)
                beside(side, UNITS)

            ffn(0, first=True)
            with dve.Fori(1, NBLK + 1) as p:
                ffn(p, side=started(mid(p - 1)))
            with dve.Fori(NBLK + 1, 2 * NBLK) as p:
                ffn(p, side=started(last(p - NBLK - 1)))
            finish(last(NBLK - 1))

        @block.tensor
        def _(pe):
            def turn(dst_bank, src, width=P):
                for t in range(BT):
                    last = nc.tensor.transpose(ps[:, dst_bank, t * P:(t + 1) * P], src(t), ident[:, :])
                return last

            def z_turn(k):
                pe.wait_ge(z_ready, BT * k + BT)
                turn(PS_B, lambda t: z[:, t, :]).then_inc(z_turned, 1)

            def attn_a(k, a, a0):
                z_turn(k)
                pe.wait_ge(zT_ready, k + 1)
                for t in range(BT):
                    n = a * BT + t
                    if t >= 2:
                        pe.wait_ge(rot_mul, 2 * n - 2)
                        pe.wait_ge(v_ready, n - 1)
                    nc.tensor.matmul(ps[:, (PS_A, PS_B)[t % 2], 0:3 * D], zT[:, t * P:(t + 1) * P], w_qkv[:, :],
                                     start=True, stop=True).then_inc(qkv_ready, 1)
                pe.wait_ge(qk_ready, BT * a + BT)
                for t in range(BT):
                    nc.tensor.transpose(ps[:, PS_A, t * P:(t + 1) * P], qk[:, t, 0, :], ident[:, :])
                for t in range(BT):
                    last = nc.tensor.matmul(ps[:, PS_B, 0:KVW], qk[:, t, 1, :], v_pad[:, t, :],
                                            start=(t == 0), stop=(t == BT - 1))
                last.then_inc(kv_turned, 1)

            def logits(k, r):
                pe.wait_ge(zT_ready, k + 1)
                for t in range(BT):
                    last = nc.tensor.matmul(ps[:, PS_A, t * E:(t + 1) * E], zT[:, t * P:(t + 1) * P], w_route[:, :],
                                            start=True, stop=True)
                last.then_inc(logits_ready, 1)

            def cw_turn(r):
                pe.wait_ge(cw_split, (r + 1) * CW_SPLITS)
                for t in range(BT):
                    last = nc.tensor.transpose(psB_bf[:, t * P:(t + 1) * P], cw_parts[:, t, :], ident_bf[:, :])
                last.then_inc(cw_turned, 1)

            def attn_b(k, b, b0):
                for t in range(BT):
                    q_t = qT[:, (b0 * BT + t) * P:(b0 * BT + t + 1) * P]
                    nc.tensor.matmul(ps[:, PS_A, t * P:(t + 1) * P], q_t, kv[:, 0:D], start=True, stop=True)
                    last = nc.tensor.matmul(ps[:, PS_B, t * HEADS:(t + 1) * HEADS], q_t, kv[:, D:KVW], start=True, stop=True)
                last.then_inc(num_ready, 1)
                pe.wait_ge(att_ready, b + 1)
                turn(PS_B, lambda t: z[:, t, :]).then_inc(att_turned, 1)
                pe.wait_ge(attT_ready, b + 1)
                for t in range(BT):
                    last = nc.tensor.matmul(ps[:, PS_A, t * P:(t + 1) * P], zT[:, t * P:(t + 1) * P], w_o[:, :],
                                            start=True, stop=True)
                last.then_inc(proj_ready, 1)
                z_turn(k)
                logits(k, b)
                cw_turn(b)

            def pre(i):
                for a0 in range(2):
                    if a0:
                        pe.wait_ge(stage_done, i * PER_BATCH + 2)
                    attn_a(i * 4 + a0, i * 2 + a0, a0)
                pe.wait_ge(stage_done, i * PER_BATCH + 4)
                for a0 in range(2):
                    attn_b(i * 4 + 2 + a0, i * 2 + a0, a0)
                    pe.wait_ge(routed, i * 2 + a0 + 1)

            pe.wait_ge(ident_ready, 2)
            pe.wait_ge(attn_loaded, 16 * N_ATTN)
            pe.wait_ge(const_loaded, 16 * N_CONST)
            with pe.Fori(0, BATCH) as i:
                pre(i)

            def mid(m):
                yield Y_TURN
                pe.wait_ge(y_out, m + 1)
                turn(PS_A, lambda t: zT[:, t * P:(t + 1) * P]).then_inc(y_turned, 1)
                yield Z1_TURN
                z_turn(8 + 2 * m)
                yield EMB
                pe.wait_ge(zT_ready, 8 + 2 * m + 1)
                nc.tensor.matmul(bank(PS_A), w_in[:, 0:D], zT[:, :], start=True, stop=True)
                nc.tensor.matmul(ps[0:SD, PS_B, :], w_in[:, D:D + SD], zT[:, :], start=True, stop=True).then_inc(emb_ps, 1)
                yield GATE
                pe.wait_ge(embT_ready, m + 1)
                pe.wait_ge(siT_ready, m + 1)
                nc.tensor.matmul(ps[0:SD, PS_A, :], w_g[:, :], embT[:, :], start=True, stop=False)
                nc.tensor.matmul(ps[0:SD, PS_A, :], w_g_s[:, :], siT[:, :], start=False, stop=True).then_inc(gate_ps, 1)
                yield MIX
                pe.wait_ge(scan_step, 4 * m + 4)
                for t in range(BT):
                    cols = slice(t * P, (t + 1) * P)
                    nc.tensor.matmul(ps[:, PS_A, cols], embT[:, cols], w_out[:, :], start=True, stop=False)
                    last = nc.tensor.matmul(ps[:, PS_A, cols], stT[:, cols], w_out_s[:, :], start=False, stop=True)
                last.then_inc(mix_ready, 1)
                yield Z2_TURN
                z_turn(8 + 2 * m + 1)
                yield LOGIT
                logits(8 + 2 * m + 1, NBLK + m)
                yield CW_TURN
                cw_turn(NBLK + m)

            def last(o):
                yield Y_TURN
                pe.wait_ge(y_out, NBLK + 1 + o)
                turn(PS_A, lambda t: zT[:, t * P:(t + 1) * P]).then_inc(out_turned, 1)

            def times(dst, w, cols, hi, lo, start, stop):
                nc.tensor.matmul(dst, W_hi[w][:, cols], hi, start=start, stop=False)
                nc.tensor.matmul(dst, W_hi[w][:, cols], lo, start=False, stop=False)
                return nc.tensor.matmul(dst, W_lo[w][:, cols], hi, start=False, stop=stop)

            def down(u, seen):
                pe.wait_ge(lo_ready, seen)
                ins = times(bank(PS_Y), 2, slice(u * P, (u + 1) * P), hid_hi[:, u % 5, :], hid_lo[:, u % 5, :],
                            u == 0, u == UNITS - 1)
                ins.then_inc(down_done, 1)

            def ffn(p, slot, first=False, side=None):
                blk = ds(slot * BLK, BLK)
                pe.wait_ge(xl_ready, p + 1)
                pe.wait_ge(routed, p + 1)
                for u in range(UNITS):
                    n = p * UNITS + u
                    cols = slice(u * P, (u + 1) * P)
                    if not first or u >= 2:
                        pe.wait_ge(silu_ready, freed(p, u))
                    times(bank(PS_G[u % 2]), 0, cols, xh[:, blk], xl[:, blk], True, True).then_inc(g_ready, 1)
                    if not first or u >= 2:
                        if u < 2:
                            pe.wait_ge(hid_ready, p * UNITS - u)
                        elif u < EU + 2:
                            pe.wait_ge(act_ready, p * EU + u - 1)
                        else:
                            pe.wait_ge(hid_ready, p * UNITS + u - 1)
                    times(bank(PS_U[u % 2]), 1, cols, xh[:, blk], xl[:, blk], True, True).then_inc(u_ready, 1)
                    if u < EU:
                        if u >= 1:
                            pe.wait_ge(hid_ready, p * UNITS + u)
                        elif not first:
                            pe.wait_ge(hid_ready, p * UNITS - (UNITS - EU))
                        nc.tensor.matmul(bank(PS_C), expert_of[:, cols], cwT[:, blk], start=True, stop=True).then_inc(c_ready, 1)
                    if u >= 2:
                        if u == 2 and not first:
                            pe.wait_ge(y_out, p)
                        down(u - 2, p * UNITS + u - 1)
                    elif not first:
                        down(UNITS - 2 + u, p * UNITS + u - 1)
                    beside(side, u)
                beside(side, UNITS)

            pe.wait_ge(piece_lo, 3 * PIECES)
            ffn(0, 0, first=True)
            with pe.Fori(1, NBLK + 1) as p:
                ffn(p, p % NBLK, side=started(mid(p - 1)))
            with pe.Fori(NBLK + 1, 2 * NBLK) as p:
                ffn(p, p % NBLK, side=started(last(p - NBLK - 1)))
            down(UNITS - 2, 2 * NBLK * UNITS - 1)
            down(UNITS - 1, 2 * NBLK * UNITS)
            finish(last(NBLK - 1))


def kernel(**inputs):
    import numpy as np
    import ml_dtypes
    import concourse.bacc as _bacc
    from concourse import mybir as _mybir
    from concourse.bass_utils import run_bass_kernel_spmd as _run

    g = {k: np.asarray(v) for k, v in inputs.items()}
    order = np.concatenate([np.arange(0, D, 2), np.arange(1, D, 2)])

    def padded(parts, rows):
        a = np.concatenate(parts, axis=0)
        full = np.zeros((HID, rows), np.float32)
        full[:a.shape[0]] = a
        return full

    gate = padded([g["L0_ffn_gate_proj"].reshape(E * I, D), g["L0_ffn_shared_gate_w"]], D).T
    up = padded([g["L0_ffn_up_proj"].reshape(E * I, D), g["L0_ffn_shared_up_w"]], D).T
    down = padded([g["L0_ffn_down_proj"].transpose(0, 2, 1).reshape(E * I, D), g["L0_ffn_shared_down_w"].T], D)
    down = down.reshape(UNITS, P, D).transpose(1, 0, 2).reshape(P, HID)

    freqs = np.float32(1.0) / np.float32(10000.0) ** (np.arange(0, HD, 2, dtype=np.float32) / np.float32(HD))
    ang = (np.arange(SEQ, dtype=np.float32)[:, None] * freqs[None, :]).astype(np.float32)
    cos = np.tile(np.cos(ang).astype(np.float32), (1, HEADS)).reshape(SEQ // P, P, D // 2).transpose(1, 0, 2)
    sin = np.tile(np.sin(ang).astype(np.float32), (1, HEADS)).reshape(SEQ // P, P, D // 2).transpose(1, 0, 2)
    head = np.arange(D // 2) // (HD // 2)
    head = np.concatenate([head, head])
    value_head = np.concatenate([np.arange(D) // HD, np.arange(HEADS)])
    expert_of = np.zeros((P, EU * P), np.float32)
    for part in range(PARTS):
        expert_of[part * E + np.arange(E * I) // I, np.arange(E * I)] = 1.0
    rows = {
        "x": g["L0_attn_a_x"].reshape(BATCH * SEQ, D),
        "w_qkv": np.concatenate([g["L0_attn_a_Wq"][:, order], g["L0_attn_a_Wk"][:, order], g["L0_attn_a_Wv"]], axis=1),
        "w_o": g["L0_attn_a_Wo"],
        "head_mask": (head[:, None] == value_head[None, :]).astype(np.float32),
        "cos": cos,
        "sin": np.stack([sin, -sin], axis=2),
        "w_route": g["L0_ffn_gate_w"].T,
        "bias_route": np.repeat(g["L0_ffn_gate_bias"][None, :], P, axis=0),
        "thr_e": np.repeat(np.arange(E, dtype=np.float32)[None, :] - (E - 1 - TOPK), P, axis=0),
        "thr_g": np.repeat(np.arange(GROUPS, dtype=np.float32)[None, :] - (GROUPS - 1 - TOPG), P, axis=0),
        "lower_e": np.repeat(np.tril(np.ones((E, E), np.float32), -1)[None], P, axis=0).astype(ml_dtypes.bfloat16),
        "lower_g": np.repeat(np.tril(np.ones((GROUPS, GROUPS), np.float32), -1)[None], P, axis=0),
        "b_in": g["L0_attn_b_b_in"][:D, None],
        "b_in_s": g["L0_attn_b_b_in"][D:, None],
        "w_in": g["L0_attn_b_W_in"],
        "w_g": g["L0_attn_b_W_g"][:D],
        "w_g_s": g["L0_attn_b_W_g"][D:],
        "b_g": g["L0_attn_b_b_g"][:, None],
        "w_out": g["L0_attn_b_W_out"][:D],
        "w_out_s": np.concatenate([g["L0_attn_b_W_out"][D:], g["L0_attn_b_b_out"][None, :]], axis=0),
        "keep": np.repeat((np.arange(1, NBLK + 1) % (SEQ // BLK) != 0).astype(np.float32)[None, :], SD, axis=0),
        "neg_half": np.full((P, BT), -0.5, np.float32),
        "expert_of": expert_of.astype(ml_dtypes.bfloat16),
        "gate_proj": gate,
        "up_proj": up,
        "down_proj": down,
    }
    nc = _bacc.Bacc("TRN2", target_bir_lowering=False, num_devices=1)
    arrays, args = {}, {}
    for name, a in rows.items():
        a = np.ascontiguousarray(a)
        arrays[f"{name}_dram"] = a
        args[name] = nc.dram_tensor(f"{name}_dram", a.shape, _mybir.dt.from_np(a.dtype), kind="ExternalInput").ap()
    out = nc.dram_tensor("out_dram", (BATCH * SEQ, D), _mybir.dt.float32, kind="ExternalOutput").ap()
    hybrid_kernel(nc, args, out)
    r = _run(nc, [arrays], core_ids=[0])
    return r.results[0]["out_dram"].reshape(BATCH, SEQ, D)
```

```python
import concourse.bass as bass
from concourse import mybir
from contextlib import ExitStack

P = 128
BATCH, SEQ, D = 2, 1024, 128
TILES = BATCH * SEQ // P
BT = 4
BLK = BT * P
NBLK = TILES // BT
HEADS, HD = 16, 8
E, I, NS = 16, 176, 2
GROUPS, TOPG, TOPK = 4, 2, 4
GE = E // GROUPS
HALVES = 2
EH = E // HALVES
BAND = P // EH
HU = I // BAND
EU = HALVES * HU
SHARED = I * NS
UNITS = EU + -(-SHARED // P)
HID = UNITS * P
SHARED_AT = (0, HU + 1, 2 * HU + 2)
HALF_AT = (1, HU + 2)
SD = 8
KVW = D + HEADS
LN_EPS, DEN_EPS, TOPK_EPS = 1e-5, 1e-6, 1e-20
PARTS = 3
WCH = 5
PIECES = UNITS // WCH
RING = 3

LAG = 3
HBUF = 5

R_STATS, R_POW, R_Z, R_TURN, R_OUT, R_LO, R_LOGIT, R_SCORE, R_TURN_CW, R_CW_OUT = 0, 1, 3, 4, 5, 6, 6, 7, 22, 23
R_RANK = (8, 9, 10, 12, 13, 15, 16, 18, 19)
B_NUM, B_DEN, B_TURN, B_OUT, B_PROJ, B_SUM = 8, 9, 12, 13, 14, 15
M_TURN, M_SUM, M_STATS, M_POW, M_Z, M_TURN_Z, M_OUT = 0, 1, 2, 3, 5, 6, 7
M_EMB, M_EMB_OUT, M_GATE, M_SIG, M_SCAN, M_MIX, M_X = 8, 9, 11, 12, 14, 17, 18
Y_OUT = LAG - 1
O_TURN, O_SUM, O_TURN2, O_SUM2 = 0, 1, 6, 7


def hybrid_kernel(nc, A, out):
    f32, f32r, bf16 = mybir.dt.float32, mybir.dt.float32r, mybir.dt.bfloat16
    ALU, ACT, AX = mybir.AluOpType, mybir.ActivationFunctionType, mybir.AxisListType
    ds = bass.ds
    ctx = ExitStack()
    with ctx:
        def sb(name, shape, dt=f32):
            return ctx.enter_context(nc.sbuf_tensor(name, shape, dt))

        def sem(name):
            return ctx.enter_context(nc.semaphore(name))

        W_hi = [sb(f"{n}_hi", [P, HID], f32r) for n in ("gate_proj", "up_proj", "down_proj")]
        W_lo = [sb(f"{n}_lo", [P, HID], f32r) for n in ("gate_proj", "up_proj", "down_proj")]
        stage = sb("stage", [P, RING, WCH * P])
        xh = sb("xh", [P, NBLK * BLK], f32r)
        xl = sb("xl", [P, NBLK * BLK], f32r)
        cwT = sb("cwT", [P, NBLK * BLK], bf16)
        expert_of = sb("expert_of", [P, HALVES * P], bf16)
        x_tok = sb("x_tok", [P, TILES, D])
        silu_sb = sb("silu_sb", [P, 2, BLK])
        act_sb = sb("act_sb", [P, 2, BLK])
        hid_sb = sb("hid_sb", [P, 2, BLK])
        hid_hi = sb("hid_hi", [P, 5, BLK], f32r)
        hid_lo = sb("hid_lo", [P, 5, BLK], f32r)
        w_qkv = sb("w_qkv", [P, 3 * D])
        w_o = sb("w_o", [P, D])
        cos_t = sb("cos_t", [P, SEQ // P, D // 2])
        sin_t = sb("sin_t", [P, SEQ // P, 2, D // 2])
        head_mask = sb("head_mask", [P, KVW])
        rot_a = sb("rot_a", [P, 2, 2, 2, D // 2])
        rot_b = sb("rot_b", [P, 2, 2, 2, D // 2])
        rot = sb("rot", [P, 2, 2, 2, D // 2])
        qk = sb("qk", [P, BT, 2, D])
        v_pad = sb("v_pad", [P, BT, KVW])
        qT = sb("qT", [P, NBLK * BLK])
        kv_half = sb("kv_half", [P, KVW])
        kv_sum = sb("kv_sum", [P, KVW])
        kv = sb("kv", [P, BATCH, KVW])
        den = sb("den", [P, BT * HEADS])
        rden = sb("rden", [P, BT * HEADS])
        xcur = sb("xcur", [P, BT, D])
        z = sb("z", [P, BT, D])
        zT = sb("zT", [P, BLK])
        yT = sb("yT", [P, BLK])
        zr = sb("zr", [P, BT, D])
        zrT = sb("zrT", [P, BLK])
        w_in = sb("w_in", [P, D + SD])
        b_in = sb("b_in", [P, 1])
        b_in_s = sb("b_in_s", [SD, 1])
        w_g = sb("w_g", [P, SD])
        w_g_s = sb("w_g_s", [SD, SD])
        b_g = sb("b_g", [SD, 1])
        w_out = sb("w_out", [P, D])
        w_out_s = sb("w_out_s", [SD + 1, D])
        embT = qk[:, 0:2, :, :].rearrange("p t a d -> p (t a d)")
        siT = rot_a[0:SD].rearrange("p t a b d -> p (t a b d)")
        gT = rot_b[0:SD].rearrange("p t a b d -> p (t a b d)")
        omgT = rot[0:SD].rearrange("p t a b d -> p (t a b d)")
        inT = qT[0:SD, 0:BLK]
        stT = sb("stT", [SD + 1, BLK])
        carry = sb("carry", [SD, 1])
        keep = sb("keep", [SD, NBLK])
        w_route = sb("w_route", [P, E])
        bias_route = sb("bias_route", [P, E])
        lower_g = sb("lower_g", [P, GROUPS, GROUPS])
        tile_inner = sb("tile_inner", [P, BT * E])
        thr_g = sb("thr_g", [P, GROUPS])
        scores = sb("scores", [P, BT, E])
        sfc = sb("sfc", [P, BT, E])
        pair_hi = sb("pair_hi", [P, BT * E // 2])
        pair_lo = sb("pair_lo", [P, BT * E // 2])
        quad = sb("quad", [P, 5, BT * GROUPS])
        beats_g = sb("beats_g", [P, BT, GROUPS, GROUPS])
        rank_g = sb("rank_g", [P, 4, BT * GROUPS])
        masked = sb("masked", [P, BT, E])
        best = sb("best", [P, BT, 8])
        above = sb("above", [P, BT, E])
        level = sb("level", [P, BT, E])
        tied = sb("tied", [P, 4, BT * E])
        chosen = sb("chosen", [P, BT * E])
        wsum = sb("wsum", [P, 4, BT])
        cw = sb("cw", [P, BT, E])
        cw_left = sb("cw_left", [P, 2, BT, E])
        cw_parts = sb("cw_parts", [P, BT, P], bf16)
        ident = sb("ident", [P, P])
        ident_bf = sb("ident_bf", [P, P], bf16)
        neg_half = sb("neg_half", [P, SEQ // P])

        class Norm:
            def __init__(self, name, n):
                self.n = n
                self.stats = sb(f"{name}_stats", [P, n, 6])
                self.mv = sb(f"{name}_mv", [P, 5, n])
                self.mean = sb(f"{name}_mean", [P, n])
                self.vpe = sb(f"{name}_vpe", [P, n])
                self.rstd = sb(f"{name}_rstd", [P, n])
                self.stats_ready, self.mv_ready = sem(f"{name}_stats_ready"), sem(f"{name}_mv_ready")
                self.vpe_ready, self.rstd_ready = sem(f"{name}_vpe_ready"), sem(f"{name}_rstd_ready")
                self.z_ready = sem(f"{name}_z_ready")

        attn_ln, route_ln, rec_ln = Norm("attn", SEQ // P), Norm("route", BT), Norm("rec", BT)

        ps = ctx.enter_context(nc.psum_tensor("ps", [P, 8, BLK], f32))
        PS_G, PS_U, PS_C, PS_Y, PS_A, PS_B = (0, 1), (2, 3), 4, 5, 6, 7

        def bank(b):
            return ps[:, b, :]

        def tiles(b):
            return ps[:, b, :].rearrange("p (t d) -> p t d", t=BT)

        psB_bf = ps[:, PS_B, 0:BLK // 2].bitcast(bf16)

        x_loaded, attn_loaded, const_loaded = sem("x_loaded"), sem("attn_loaded"), sem("const_loaded")
        piece_loaded = [sem(f"piece_loaded{i}") for i in range(RING)]
        piece_hi, piece_lo = sem("piece_hi"), sem("piece_lo")
        ident_zero, ident_ready = sem("ident_zero"), sem("ident_ready")
        z_turned, zT_ready, qkv_ready, rot_mul = sem("z_turned"), sem("zT_ready"), sem("qkv_ready"), sem("rot_mul")
        rot_ready, v_ready, qk_ready, kv_turned = sem("rot_ready"), sem("v_ready"), sem("qk_ready"), sem("kv_turned")
        qT_ready, kv_out, kv_summed, kv_ready = sem("qT_ready"), sem("kv_out"), sem("kv_summed"), sem("kv_ready")
        num_ready, den_ready, rden_ready, att_ready = sem("num_ready"), sem("den_ready"), sem("rden_ready"), sem("att_ready")
        att_turned, attT_ready, proj_ready, x_ready = sem("att_turned"), sem("attT_ready"), sem("proj_ready"), sem("x_ready")
        zr_turned, zrT_ready, xh_ready, xl_ready = sem("zr_turned"), sem("zrT_ready"), sem("xh_ready"), sem("xl_ready")
        logits_ready, scores_ready, route_step = sem("logits_ready"), sem("scores_ready"), sem("route_step")
        cw_split, cw_turned, routed = sem("cw_split"), sem("cw_turned"), sem("routed")
        g_ready, u_ready, c_ready = sem("g_ready"), sem("u_ready"), sem("c_ready")
        silu_ready, act_ready, hid_ready = sem("silu_ready"), sem("act_ready"), sem("hid_ready")
        hi_ready, lo_ready, down_done, y_out = sem("hi_ready"), sem("lo_ready"), sem("down_done"), sem("y_out")
        y_turned, xcur_ready, zm_turned, zmT_ready = sem("y_turned"), sem("xcur_ready"), sem("zm_turned"), sem("zmT_ready")
        emb_ps, embT_ready, siT_ready = sem("emb_ps"), sem("embT_ready"), sem("siT_ready")
        gate_ps, gT_ready, scan_step, mix_ready = sem("gate_ps"), sem("gT_ready"), sem("scan_step"), sem("mix_ready")
        out_ready, out_stored = sem("out_ready"), sem("out_stored")

        block = ctx.enter_context(nc.Block())

        ATTN_IN = ("w_qkv", "w_o", "head_mask", "cos", "sin")
        CONST_IN = ("w_route", "bias_route", "tile_inner", "thr_g", "lower_g", "expert_of", "b_in", "b_in_s",
                    "w_in", "w_g", "w_g_s", "b_g", "w_out", "w_out_s", "keep")
        place = {"w_qkv": w_qkv, "w_o": w_o, "head_mask": head_mask, "cos": cos_t, "sin": sin_t, "w_route": w_route,
                 "bias_route": bias_route, "tile_inner": tile_inner, "thr_g": thr_g, "lower_g": lower_g,
                 "expert_of": expert_of, "b_in": b_in, "b_in_s": b_in_s, "w_in": w_in, "w_g": w_g, "w_g_s": w_g_s,
                 "b_g": b_g, "w_out": w_out, "w_out_s": w_out_s, "keep": keep}
        ROUTE_STEPS, CW_SPLITS, MV_STEPS, SCAN_STEPS = 32, 2 * PARTS - 1, 6, 4
        FFN_BLOCKS = 2 * NBLK
        LAST_REC = NBLK + 1
        a_z, a_zT, a_bank = (z, zr, z, z), (zT, zrT, zT, zT), (0, 1, 0, 1)
        qkv_bank, q_bank, kv_bank = (2, 3), 4, 5

        def started(steps):
            return [steps, next(steps)]

        def beside(sides, u):
            for side in sides:
                while side[1] <= u:
                    side[1] = next(side[0], 2 * UNITS)

        def freed(p, u):
            return p * UNITS + u - 1 if u >= 2 else p * UNITS - u

        def product_done(p, u):
            w, through = (u - 2, p) if u >= 2 else (UNITS - 1 - u, p - 1)
            if w in SHARED_AT:
                return hid_ready, through * UNITS + w + 1
            return act_ready, through * EU + routed_units(w) + 1

        def routed_units(u):
            return u - sum(s < u for s in SHARED_AT)

        def attn_block(p):
            return p + 2

        def weight_piece(n):
            w, c = n % 3, n // 3
            return w, slice(c * WCH * P, (c + 1) * WCH * P)

        @block.sync
        def _(sp):
            sp.dma_start(x_tok[:, :, :], A["x"].rearrange("(t p) d -> p t d", p=P)).then_inc(x_loaded, 16)
            for name in ATTN_IN:
                sp.dma_start(place[name][:], A[name]).then_inc(attn_loaded, 16)
            for n in range(3 * PIECES):
                if n >= RING:
                    sp.wait_ge(piece_lo, n - RING + 1)
                w, cols = weight_piece(n)
                sp.dma_start(stage[:, n % RING, :], A[("gate_proj", "up_proj", "down_proj")[w]][:, cols])\
                    .then_inc(piece_loaded[n % RING], 16)
            for o in range(NBLK):
                sp.wait_ge(out_ready, o + 1)
                sp.dma_start(out.rearrange("(b t p) d -> b p t d", p=P, t=BT)[o], xcur[:, :, :]).then_inc(out_stored, 16)
            sp.wait_ge(out_stored, 16 * NBLK)

        @block.gpsimd
        def _(pool):
            nc.gpsimd.memset(ident[:, :], 0.0).then_inc(ident_zero, 1)
            nc.gpsimd.memset(neg_half[:, :], -0.5)
            nc.gpsimd.memset(v_pad[:, :, :], 1.0)
            nc.gpsimd.memset(cw_parts[:, :, :], 0.0)
            nc.gpsimd.memset(stT[:, :], 1.0)
            nc.gpsimd.memset(carry[:, :], 0.0)
            pool.wait_ge(ident_zero, 1)
            nc.gpsimd.affine_select(out=ident[:, :], in_=ident[:, :], compare_op=ALU.not_equal, fill=1.0,
                                    base=0, pattern=[[-1, P]], channel_multiplier=1).then_inc(ident_ready, 1)
            pool.wait_ge(ident_ready, 1)
            nc.gpsimd.tensor_copy(ident_bf[:, :], ident[:, :]).then_inc(ident_ready, 1)

            def rstd(ln, k):
                pool.wait_ge(ln.vpe_ready, k + 1)
                nc.gpsimd.tensor_tensor(ln.rstd[:, :], ln.vpe[:, :], neg_half[:, 0:ln.n], ALU.pow).then_inc(ln.rstd_ready, 1)

            def rotate(a, t):
                n = a * BT + t
                pool.wait_ge(rot_mul, 2 * n + 2)
                if n >= 2:
                    pool.wait_ge(qk_ready, n - 1)
                nc.gpsimd.tensor_tensor(rot[:, t % 2, :, 0, :], rot_a[:, t % 2, :, 0, :],
                                        rot_b[:, t % 2, :, 1, :], ALU.add)
                nc.gpsimd.tensor_tensor(rot[:, t % 2, :, 1, :], rot_a[:, t % 2, :, 1, :],
                                        rot_b[:, t % 2, :, 0, :], ALU.add).then_inc(rot_ready, 1)

            def weight_lo(n):
                w, cols = weight_piece(n)
                pool.wait_ge(piece_hi, n + 1)
                nc.gpsimd.tensor_tensor(W_lo[w][:, cols], stage[:, n % RING, :], W_hi[w][:, cols].bitcast(f32),
                                        ALU.subtract).then_inc(piece_lo, 1)

            def route(r, slot):
                yield R_POW
                rstd(route_ln, r)
                yield R_LO
                pool.wait_ge(xh_ready, r + 1)
                nc.gpsimd.tensor_tensor(xl[:, ds(slot * BLK, BLK)], zrT[:, :],
                                        xh[:, ds(slot * BLK, BLK)].bitcast(f32), ALU.subtract).then_inc(xl_ready, 1)

            def recur(m):
                yield M_POW
                rstd(rec_ln, m)

            def ffn(p, sides):
                for u in range(UNITS):
                    pool.wait_ge(hi_ready, p * UNITS + u + 1)
                    nc.gpsimd.tensor_tensor(hid_lo[:, u % HBUF, :], hid_sb[:, u % 2, :],
                                            hid_hi[:, u % HBUF, :].bitcast(f32), ALU.subtract).then_inc(lo_ready, 1)
                    beside(sides, u)

            rstd(attn_ln, 0)
            rstd(attn_ln, 1)
            for a in range(2):
                for t in range(BT):
                    rotate(a, t)
            r0 = started(route(0, 0))
            for n in range(3):
                weight_lo(n)
            for t in range(BT):
                rotate(2, t)
            weight_lo(3)
            beside([r0], R_POW)
            weight_lo(4)
            beside([r0], R_LO)
            for t in range(BT):
                rotate(3, t)
            for n in range(5, 3 * PIECES):
                weight_lo(n)
            ffn(0, [started(route(1, 1))])
            ffn(1, [started(route(2, 2))])
            with pool.Fori(2, LAST_REC + 1) as p:
                ffn(p, [started(route(p + 1, (p + 1) % NBLK)), started(recur(p - 2))])
            ffn(FFN_BLOCKS - 2, [started(route(FFN_BLOCKS - 1, NBLK - 1))])
            ffn(FFN_BLOCKS - 1, [])

        @block.scalar
        def _(act):
            for name in CONST_IN:
                act.dma_start(place[name][:], A[name]).then_inc(const_loaded, 16)

            def turned(a):
                act.wait_ge(z_turned, a + 1)
                nc.scalar.activation(a_zT[a][:, :], bank(a_bank[a]), ACT.Copy).then_inc(zT_ready, 1)

            def values(a, t):
                n = a * BT + t
                src = bank(qkv_bank[t % 2])
                if a and t == 0:
                    act.wait_ge(kv_turned, a)
                act.wait_ge(rot_mul, 2 * n + 2)
                nc.scalar.activation(v_pad[:, t, 0:D], src[:, 2 * D:3 * D], ACT.Copy).then_inc(v_ready, 1)
                act.wait_ge(rot_ready, n + 1)
                nc.scalar.activation(qk[:, t, :, :], rot[:, t % 2, :, :, :].rearrange("p a b d -> p a (b d)"),
                                     ACT.Relu).then_inc(qk_ready, 1)

            def queries(a):
                act.wait_ge(kv_turned, a + 1)
                nc.scalar.activation(qT[:, a * BLK:(a + 1) * BLK], bank(q_bank), ACT.Copy).then_inc(qT_ready, 1)

            def weight_hi(n):
                w, cols = weight_piece(n)
                act.wait_ge(piece_loaded[n % RING], 16 * (n // RING + 1))
                nc.scalar.activation(W_hi[w][:, cols], stage[:, n % RING, :], ACT.Copy).then_inc(piece_hi, 1)

            def attend(b, attT):
                yield B_OUT
                act.wait_ge(att_turned, b + 1)
                nc.scalar.activation(attT[:, :], bank(PS_A), ACT.Copy).then_inc(attT_ready, 1)

            def route(r, slot):
                yield R_OUT
                act.wait_ge(zr_turned, r + 1)
                nc.scalar.activation(zrT[:, :], bank(PS_B), ACT.Copy).then_inc(zrT_ready, 1)
                nc.scalar.activation(xh[:, ds(slot * BLK, BLK)], bank(PS_B), ACT.Copy).then_inc(xh_ready, 1)
                yield R_SCORE
                act.wait_ge(logits_ready, r + 1)
                nc.scalar.activation(scores[:, :, :].rearrange("p t e -> p (t e)"), ps[:, PS_B, 0:BT * E],
                                     ACT.Sigmoid).then_inc(scores_ready, 1)
                yield R_CW_OUT
                act.wait_ge(cw_turned, r + 1)
                act.wait_ge(xl_ready, r + 1)
                nc.scalar.activation(cwT[:, ds(slot * BLK, BLK)], psB_bf, ACT.Copy).then_inc(routed, 1)

            def y_copy(p, turned_before):
                act.wait_ge(down_done, p * UNITS)
                if turned_before:
                    act.wait_ge(y_turned, p - 1)
                nc.scalar.activation(yT[:, :], bank(PS_Y), ACT.Copy).then_inc(y_out, 1)

            def leave(p, turned_before=True):
                yield Y_OUT
                y_copy(p, turned_before)

            def recur(m):
                yield M_OUT
                act.wait_ge(zm_turned, m + 1)
                nc.scalar.activation(zT[:, :], bank(PS_A), ACT.Copy).then_inc(zmT_ready, 1)
                yield M_EMB_OUT
                act.wait_ge(emb_ps, m + 1)
                nc.scalar.activation(embT, bank(PS_A), ACT.Identity, bias=b_in[:, 0:1]).then_inc(embT_ready, 1)
                yield M_SIG
                act.wait_ge(gate_ps, m + 1)
                nc.scalar.activation(gT, ps[0:SD, PS_A, :], ACT.Sigmoid, bias=b_g[:, 0:1]).then_inc(gT_ready, 1)

            def hid_high(p, u, first):
                act.wait_ge(hid_ready, p * UNITS + u + 1)
                if not first or u >= HBUF:
                    act.wait_ge(down_done, p * UNITS + u + 1 - HBUF)
                nc.scalar.activation(hid_hi[:, u % HBUF, :], hid_sb[:, u % 2, :], ACT.Copy).then_inc(hi_ready, 1)

            def ffn(p, sides, first=False):
                for u in range(UNITS):
                    act.wait_ge(g_ready, p * UNITS + u + 1)
                    if not first or u >= 2:
                        act.wait_ge(*product_done(p, u))
                    nc.scalar.activation(silu_sb[:, u % 2, :], bank(PS_G[u % 2]), ACT.Silu).then_inc(silu_ready, 1)
                    if u >= 1:
                        hid_high(p, u - 1, first)
                    beside(sides, u)
                hid_high(p, UNITS - 1, first)

            act.wait_ge(ident_ready, 2)
            turned(0)
            turned(1)
            for a in range(2):
                for t in range(BT):
                    values(a, t)
                queries(a)
            r0, b0, b1 = started(route(0, 0)), started(attend(0, yT)), started(attend(1, yT))
            for n in range(3):
                weight_hi(n)
            turned(2)
            values(2, 0)
            values(2, 1)
            beside([b0], B_OUT)
            values(2, 2)
            values(2, 3)
            queries(2)
            weight_hi(3)
            turned(3)
            beside([r0], R_OUT)
            weight_hi(4)
            values(3, 0)
            values(3, 1)
            beside([r0], R_SCORE)
            values(3, 2)
            values(3, 3)
            queries(3)
            weight_hi(5)
            beside([b1], B_OUT)
            for n in range(6, 10):
                weight_hi(n)
            beside([r0], R_CW_OUT)
            for n in range(10, 3 * PIECES):
                weight_hi(n)
            act.wait_ge(const_loaded, 16 * len(CONST_IN))
            ffn(0, [started(route(1, 1)), started(attend(attn_block(0), zT))], first=True)
            ffn(1, [started(leave(1, False)), started(route(2, 2)), started(attend(attn_block(1), zT))])
            with act.Fori(2, LAST_REC + 1) as p:
                ffn(p, [started(leave(p)), started(route(p + 1, (p + 1) % NBLK)), started(recur(p - 2))])
            ffn(FFN_BLOCKS - 2, [started(leave(FFN_BLOCKS - 2)), started(route(FFN_BLOCKS - 1, NBLK - 1))])
            ffn(FFN_BLOCKS - 1, [started(leave(FFN_BLOCKS - 1))])
            y_copy(FFN_BLOCKS, True)

        @block.vector
        def _(dve):
            def norm_stats(ln, k, src):
                for t in range(ln.n):
                    nc.vector.bn_stats(ln.stats[:, t, :], src(t)).then_inc(ln.stats_ready, 1)
                stats, mv = ln.stats, ln.mv
                dve.wait_ge(ln.stats_ready, ln.n * k + ln.n)
                nc.vector.tensor_tensor(mv[:, 0, :], stats[:, :, 1], stats[:, :, 4], ALU.add).then_inc(ln.mv_ready, 1)
                nc.vector.tensor_tensor(mv[:, 1, :], stats[:, :, 1], stats[:, :, 4], ALU.subtract).then_inc(ln.mv_ready, 1)
                nc.vector.tensor_tensor(mv[:, 2, :], stats[:, :, 2], stats[:, :, 5], ALU.add).then_inc(ln.mv_ready, 1)
                dve.wait_ge(ln.mv_ready, MV_STEPS * k + 3)
                nc.vector.scalar_tensor_tensor(out=mv[:, 3, :], in0=mv[:, 1, :], scalar=0.25, in1=mv[:, 1, :],
                                               op0=ALU.mult, op1=ALU.mult).then_inc(ln.mv_ready, 1)
                nc.vector.tensor_scalar(mv[:, 4, :], mv[:, 2, :], 1.0 / D, LN_EPS, ALU.mult, ALU.add).then_inc(ln.mv_ready, 1)
                nc.vector.tensor_scalar(ln.mean[:, :], mv[:, 0, :], 0.5, None, ALU.mult).then_inc(ln.mv_ready, 1)
                dve.wait_ge(ln.mv_ready, MV_STEPS * k + 6)
                nc.vector.tensor_tensor(ln.vpe[:, :], mv[:, 3, :], mv[:, 4, :], ALU.add).then_inc(ln.vpe_ready, 1)

            def norm(ln, k, dst, src, t0=0):
                dve.wait_ge(ln.rstd_ready, k + 1)
                for t in range(BT):
                    nc.vector.tensor_scalar(dst[:, t, :], src(t), ln.mean[:, t0 + t:t0 + t + 1],
                                            ln.rstd[:, t0 + t:t0 + t + 1], ALU.subtract, ALU.mult).then_inc(ln.z_ready, 1)

            def tile_of(b):
                def src(t):
                    return x_tok[:, ds(b * BT + t, 1), :].rearrange("p t d -> p (t d)")
                return src

            def attn_stats(i):
                norm_stats(attn_ln, i, lambda t: x_tok[:, i * SEQ // P + t, :])

            def attn_norm(a):
                if a >= 2:
                    dve.wait_ge(z_turned, a if a == 3 else 1)
                norm(attn_ln, a // 2, a_z[a], lambda t: x_tok[:, a * BT + t, :], a % 2 * BT)

            def rotate(a, t):
                n, pos = a * BT + t, a % 2 * BT + t
                pst = ps[:, qkv_bank[t % 2], 0:2 * D].rearrange("p (a b d) -> p a b d", a=2, b=2)
                dve.wait_ge(qkv_ready, n + 1)
                if n >= 2:
                    dve.wait_ge(rot_ready, n - 1)
                nc.vector.tensor_tensor(
                    rot_a[:, t % 2].rearrange("p a b d -> p (a b) d"), pst.rearrange("p a b d -> p (a b) d"),
                    cos_t[:, pos:pos + 1, :].to_broadcast([P, 4, D // 2]), ALU.mult).then_inc(rot_mul, 1)
                nc.vector.tensor_tensor(
                    rot_b[:, t % 2], pst,
                    sin_t[:, pos:pos + 1, :, :].to_broadcast([P, 2, 2, D // 2]), ALU.mult).then_inc(rot_mul, 1)

            def sum_kv(a):
                dve.wait_ge(kv_turned, a + 1)
                if a % 2 == 0:
                    nc.vector.tensor_copy(kv_half[:, :], ps[:, kv_bank, 0:KVW]).then_inc(kv_out, 1)
                else:
                    i = a // 2
                    dve.wait_ge(kv_out, 2 * i + 1)
                    nc.vector.tensor_tensor(kv_sum[:, :], ps[:, kv_bank, 0:KVW], kv_half[:, :], ALU.add).then_inc(kv_out, 1)
                    dve.wait_ge(kv_out, 2 * i + 2)
                    nc.vector.tensor_tensor(kv[:, i, :], kv_sum[:, :], head_mask[:, :], ALU.mult).then_inc(kv_ready, 1)

            def attend(b):
                yield B_DEN
                dve.wait_ge(num_ready, b + 1)
                nc.vector.tensor_scalar(den[:, :], ps[:, PS_B, 0:BT * HEADS], DEN_EPS, None, ALU.add).then_inc(den_ready, 1)
                dve.wait_ge(den_ready, b + 1)
                nc.vector.reciprocal(rden[:, :], den[:, :]).then_inc(rden_ready, 1)
                dve.wait_ge(rden_ready, b + 1)
                nc.vector.tensor_tensor(xcur[:, :, :].rearrange("p t (h e) -> p (t h) e", h=HEADS),
                                        bank(PS_A).rearrange("p (h e) -> p h e", e=HD),
                                        rden[:, :, None].to_broadcast([P, BT * HEADS, HD]), ALU.mult).then_inc(att_ready, 1)
                yield B_SUM
                dve.wait_ge(proj_ready, b + 1)
                nc.vector.tensor_tensor(x_tok[:, b * BT:(b + 1) * BT, :], tiles(PS_A), x_tok[:, b * BT:(b + 1) * BT, :],
                                        ALU.add).then_inc(x_ready, 1)

            def route(r, b):
                yield R_STATS
                dve.wait_ge(x_ready, r + 1)
                norm_stats(route_ln, r, tile_of(b))
                yield R_Z
                norm(route_ln, r, zr, tile_of(b))
                yield R_RANK[0]
                dve.wait_ge(scores_ready, r + 1)
                done = [0]

                def step(ins):
                    done[0] += 1
                    ins.then_inc(route_step, 1)

                def after(n):
                    dve.wait_ge(route_step, r * ROUTE_STEPS + n)

                def tt(o, a, b, op):
                    step(nc.vector.tensor_tensor(o, a, b, op))

                tt(sfc[:, :, :], scores[:, :, :], bias_route[:, None, :].to_broadcast([P, BT, E]), ALU.add)
                after(1)
                pairs = sfc[:, :, :].rearrange("p t (g two) -> p (t g) two", two=2)
                tt(pair_hi[:, :], pairs[:, :, 0], pairs[:, :, 1], ALU.max)
                tt(pair_lo[:, :], pairs[:, :, 0], pairs[:, :, 1], ALU.min)
                hi2 = pair_hi[:, :].rearrange("p (g two) -> p g two", two=2)
                lo2 = pair_lo[:, :].rearrange("p (g two) -> p g two", two=2)
                after(3)
                tt(quad[:, 0, :], hi2[:, :, 0], hi2[:, :, 1], ALU.max)
                tt(quad[:, 1, :], hi2[:, :, 0], hi2[:, :, 1], ALU.min)
                tt(quad[:, 2, :], lo2[:, :, 0], lo2[:, :, 1], ALU.max)
                yield R_RANK[1]
                after(6)
                tt(quad[:, 3, :], quad[:, 1, :], quad[:, 2, :], ALU.max)
                after(7)
                tt(quad[:, 4, :], quad[:, 0, :], quad[:, 3, :], ALU.add)
                after(8)
                gs = quad[:, 4, :].rearrange("p (t g) -> p t g", t=BT)
                tt(beats_g[:, :, :, :], gs[:, :, None, :].to_broadcast([P, BT, GROUPS, GROUPS]),
                   gs[:, :, :, None].to_broadcast([P, BT, GROUPS, GROUPS]), ALU.is_ge)
                after(9)
                tt(beats_g[:, :, :, :], beats_g[:, :, :, :],
                   lower_g[:, None, :, :].to_broadcast([P, BT, GROUPS, GROUPS]), ALU.mult)
                yield R_RANK[2]
                after(10)
                step(nc.vector.tensor_reduce(rank_g[:, 0, :], beats_g[:, :, :, :].rearrange("p t i j -> p (t i) j"),
                                             AX.X, ALU.add))
                step(nc.vector.tensor_reduce(rank_g[:, 1, :].rearrange("p (t i) -> p t i", t=BT),
                                             beats_g[:, :, :, :].rearrange("p t i j -> p t j i"), AX.X, ALU.add))
                after(12)
                tt(rank_g[:, 2, :], rank_g[:, 0, :], rank_g[:, 1, :], ALU.subtract)
                after(13)
                tt(rank_g[:, 3, :].rearrange("p (t g) -> p t g", t=BT), rank_g[:, 2, :].rearrange("p (t g) -> p t g", t=BT),
                   thr_g[:, None, :].to_broadcast([P, BT, GROUPS]), ALU.is_lt)
                yield R_RANK[3]
                after(14)
                tt(masked[:, :, :].rearrange("p t (g e) -> p (t g) e", e=GE),
                   sfc[:, :, :].rearrange("p t (g e) -> p (t g) e", e=GE),
                   rank_g[:, 3, :, None].to_broadcast([P, BT * GROUPS, GE]), ALU.mult)
                after(15)
                tt(tied[:, 0, :], masked[:, :, :].rearrange("p t e -> p (t e)"), tile_inner[:, :], ALU.mult)
                for t in range(BT):
                    step(nc.vector.max(best[:, t, :], masked[:, t, :]))
                yield R_RANK[4]
                after(20)
                fourth = best[:, :, TOPK - 1:TOPK].to_broadcast([P, BT, E])
                tt(above[:, :, :], masked[:, :, :], fourth, ALU.is_gt)
                tt(level[:, :, :], masked[:, :, :], fourth, ALU.is_equal)
                after(22)
                step(nc.vector.tensor_reduce(wsum[:, 3, :], above[:, :, :], AX.X, ALU.add))
                step(nc.vector.tensor_tensor_scan(tied[:, 1, :], tile_inner[:, :], level[:, :, :].rearrange("p t e -> p (t e)"),
                                                  0.0, ALU.mult, ALU.add))
                yield R_RANK[5]
                after(24)
                tt(tied[:, 2, :].rearrange("p (t e) -> p t e", t=BT), tied[:, 1, :].rearrange("p (t e) -> p t e", t=BT),
                   wsum[:, 3, :, None].to_broadcast([P, BT, E]), ALU.add)
                after(25)
                step(nc.vector.scalar_tensor_tensor(out=tied[:, 3, :], in0=tied[:, 2, :], scalar=float(TOPK),
                                                    in1=level[:, :, :].rearrange("p t e -> p (t e)"),
                                                    op0=ALU.is_le, op1=ALU.mult))
                after(26)
                tt(chosen[:, :], tied[:, 3, :], above[:, :, :].rearrange("p t e -> p (t e)"), ALU.add)
                yield R_RANK[6]
                after(27)
                tt(masked[:, :, :], scores[:, :, :], chosen[:, :].rearrange("p (t e) -> p t e", t=BT), ALU.mult)
                after(28)
                step(nc.vector.tensor_reduce(wsum[:, 0, :], masked[:, :, :], AX.X, ALU.add))
                yield R_RANK[7]
                after(29)
                step(nc.vector.tensor_scalar(wsum[:, 1, :], wsum[:, 0, :], TOPK_EPS, None, ALU.add))
                after(30)
                step(nc.vector.reciprocal(wsum[:, 2, :], wsum[:, 1, :]))
                after(31)
                tt(cw[:, :, :], masked[:, :, :], wsum[:, 2, :, None].to_broadcast([P, BT, E]), ALU.mult)
                yield R_RANK[8]
                after(32)
                assert done[0] == ROUTE_STEPS
                left = cw[:, :, :]
                for part in range(PARTS):
                    here = cw_parts[:, :, part * E:(part + 1) * E]
                    nc.vector.tensor_copy(here, left).then_inc(cw_split, 1)
                    dve.wait_ge(cw_split, r * CW_SPLITS + 2 * part + 1)
                    if part < PARTS - 1:
                        nc.vector.tensor_tensor(cw_left[:, part, :, :], left, here, ALU.subtract).then_inc(cw_split, 1)
                        dve.wait_ge(cw_split, r * CW_SPLITS + 2 * part + 2)
                        left = cw_left[:, part, :, :]

            def recur(m):
                def cur(t):
                    return xcur[:, t, :]
                yield M_SUM
                dve.wait_ge(y_turned, m + 1)
                nc.vector.tensor_tensor(xcur[:, :, :], tiles(PS_A), x_tok[:, ds(m * BT, BT), :], ALU.add).then_inc(xcur_ready, 1)
                yield M_STATS
                dve.wait_ge(xcur_ready, m + 1)
                norm_stats(rec_ln, m, cur)
                yield M_Z
                norm(rec_ln, m, z, cur)
                yield M_EMB_OUT
                dve.wait_ge(emb_ps, m + 1)
                nc.vector.tensor_scalar(siT, ps[0:SD, PS_B, :], b_in_s[:, 0:1], None, ALU.add).then_inc(siT_ready, 1)
                yield M_SCAN
                dve.wait_ge(gT_ready, m + 1)
                nc.vector.tensor_scalar(omgT, gT, -1.0, 1.0, ALU.mult, ALU.add).then_inc(scan_step, 1)
                dve.wait_ge(scan_step, SCAN_STEPS * m + 1)
                nc.vector.tensor_tensor(inT, omgT, siT, ALU.mult).then_inc(scan_step, 1)
                yield M_SCAN + 1
                dve.wait_ge(scan_step, SCAN_STEPS * m + 2)
                nc.vector.tensor_tensor_scan(stT[0:SD, :], gT, inT, carry[:, 0:1], ALU.mult, ALU.add).then_inc(scan_step, 1)
                dve.wait_ge(scan_step, SCAN_STEPS * m + 3)
                nc.vector.tensor_tensor(carry[:, 0:1], stT[0:SD, BLK - 1:BLK], keep[:, ds(m, 1)], ALU.mult).then_inc(scan_step, 1)
                yield M_X
                dve.wait_ge(mix_ready, m + 1)
                nc.vector.tensor_tensor(x_tok[:, ds(m * BT, BT), :], tiles(PS_A), xcur[:, :, :], ALU.add).then_inc(x_ready, 1)

            def output(o, unit=O_SUM):
                yield unit
                dve.wait_ge(y_turned, NBLK + o + 1)
                if o:
                    dve.wait_ge(out_stored, 16 * o)
                nc.vector.tensor_tensor(xcur[:, :, :], tiles(PS_A), x_tok[:, o * BT:(o + 1) * BT, :], ALU.add)\
                    .then_inc(out_ready, 1)

            def ffn(p, sides, first=False):
                for u in range(UNITS):
                    n = p * UNITS + u
                    if u >= 1 and u - 1 not in SHARED_AT:
                        if u - 1 in HALF_AT:
                            dve.wait_ge(c_ready, HALVES * p + HALF_AT.index(u - 1) + 1)
                        dve.wait_ge(act_ready, p * EU + routed_units(u))
                        if not first or u >= 3:
                            dve.wait_ge(lo_ready, freed(p, u - 1))
                        nc.vector.tensor_tensor(hid_sb[:, (u - 1) % 2, :], bank(PS_C), act_sb[:, (u - 1) % 2, :],
                                                ALU.mult).then_inc(hid_ready, 1)
                    dve.wait_ge(silu_ready, n + 1)
                    dve.wait_ge(u_ready, n + 1)
                    if u not in SHARED_AT:
                        if not first or u >= 2:
                            dve.wait_ge(hid_ready, freed(p, u))
                        dst, told = act_sb, act_ready
                    else:
                        if not first or u >= 2:
                            dve.wait_ge(lo_ready, freed(p, u))
                        dst, told = hid_sb, hid_ready
                    nc.vector.tensor_tensor(dst[:, u % 2, :], bank(PS_U[u % 2]), silu_sb[:, u % 2, :], ALU.mult).then_inc(told, 1)
                    beside(sides, u)

            dve.wait_ge(x_loaded, 16)
            attn_stats(0)
            attn_norm(0)
            attn_norm(1)
            attn_stats(1)
            dve.wait_ge(attn_loaded, 16 * len(ATTN_IN))
            for a in range(2):
                for t in range(BT):
                    rotate(a, t)
                sum_kv(a)
            r0, b0, b1 = started(route(0, 0)), started(attend(0)), started(attend(1))
            attn_norm(2)
            beside([b0], B_DEN)
            for t in range(BT):
                rotate(2, t)
            beside([b0], B_SUM)
            beside([r0], R_STATS)
            attn_norm(3)
            beside([r0], R_Z)
            sum_kv(2)
            for t in range(BT):
                rotate(3, t)
            sum_kv(3)
            dve.wait_ge(const_loaded, 16 * len(CONST_IN))
            dve.wait_ge(ident_ready, 2)
            beside([r0], R_RANK[2])
            beside([b1], B_DEN)
            beside([r0], R_RANK[-1])
            beside([b1], B_SUM)
            ffn(0, [started(route(1, 1)), started(attend(attn_block(0)))], first=True)
            ffn(1, [started(route(2, 2)), started(attend(attn_block(1)))])
            with dve.Fori(2, LAST_REC + 1) as p:
                ffn(p, [started(route(p + 1, (p + 1) % NBLK)), started(recur(p - 2))])
            ffn(FFN_BLOCKS - 2, [started(route(FFN_BLOCKS - 1, NBLK - 1)), started(output(0))])
            ffn(FFN_BLOCKS - 1, [started(output(1)), started(output(2, O_SUM2))])
            beside([started(output(3))], O_SUM)

        @block.tensor
        def _(pe):
            def turn(dst_bank, src):
                for t in range(BT):
                    last = nc.tensor.transpose(ps[:, dst_bank, t * P:(t + 1) * P], src(t), ident[:, :])
                return last

            def attn_turn(a):
                pe.wait_ge(attn_ln.z_ready, BT * (a + 1))
                turn(a_bank[a], lambda t: a_z[a][:, t, :]).then_inc(z_turned, 1)

            def attn_qkv(a, t):
                n = a * BT + t
                if t == 0:
                    pe.wait_ge(zT_ready, a + 1)
                if n >= 2:
                    pe.wait_ge(v_ready, n - 1)
                nc.tensor.matmul(ps[:, qkv_bank[t % 2], 0:3 * D], a_zT[a][:, t * P:(t + 1) * P], w_qkv[:, :],
                                 start=True, stop=True).then_inc(qkv_ready, 1)

            def attn_kv(a):
                pe.wait_ge(qk_ready, BT * (a + 1))
                if a:
                    pe.wait_ge(qT_ready, a)
                    if a % 2:
                        pe.wait_ge(kv_out, a // 2 * 2 + 1)
                    else:
                        pe.wait_ge(kv_ready, a // 2)
                for t in range(BT):
                    nc.tensor.transpose(ps[:, q_bank, t * P:(t + 1) * P], qk[:, t, 0, :], ident[:, :])
                for t in range(BT):
                    last = nc.tensor.matmul(ps[:, kv_bank, 0:KVW], qk[:, t, 1, :], v_pad[:, t, :],
                                            start=(t == 0), stop=(t == BT - 1))
                last.then_inc(kv_turned, 1)

            def attend(b, attT):
                yield B_NUM
                pe.wait_ge(qT_ready, b + 1)
                pe.wait_ge(kv_ready, b // 2 + 1)
                if b:
                    pe.wait_ge(x_ready, b)
                    pe.wait_ge(scores_ready, b)
                for t in range(BT):
                    q_t = qT[:, (b * BT + t) * P:(b * BT + t + 1) * P]
                    nc.tensor.matmul(ps[:, PS_A, t * P:(t + 1) * P], q_t, kv[:, b // 2, 0:D], start=True, stop=True)
                    last = nc.tensor.matmul(ps[:, PS_B, t * HEADS:(t + 1) * HEADS], q_t, kv[:, b // 2, D:KVW],
                                            start=True, stop=True)
                last.then_inc(num_ready, 1)
                yield B_TURN
                pe.wait_ge(att_ready, b + 1)
                turn(PS_A, lambda t: xcur[:, t, :]).then_inc(att_turned, 1)
                yield B_PROJ
                pe.wait_ge(attT_ready, b + 1)
                for t in range(BT):
                    last = nc.tensor.matmul(ps[:, PS_A, t * P:(t + 1) * P], attT[:, t * P:(t + 1) * P], w_o[:, :],
                                            start=True, stop=True)
                last.then_inc(proj_ready, 1)

            def route(r, beside_done=None, first=False):
                yield R_TURN
                pe.wait_ge(route_ln.z_ready, BT * (r + 1))
                if not first:
                    pe.wait_ge(routed, r)
                turn(PS_B, lambda t: zr[:, t, :]).then_inc(zr_turned, 1)
                yield R_LOGIT
                pe.wait_ge(zrT_ready, r + 1)
                pe.wait_ge(xh_ready, r + 1)
                for t in range(BT):
                    last = nc.tensor.matmul(ps[:, PS_B, t * E:(t + 1) * E], zrT[:, t * P:(t + 1) * P], w_route[:, :],
                                            start=True, stop=True)
                last.then_inc(logits_ready, 1)
                yield R_TURN_CW
                pe.wait_ge(cw_split, (r + 1) * CW_SPLITS)
                if beside_done:
                    pe.wait_ge(*beside_done)
                for t in range(BT):
                    last = nc.tensor.transpose(psB_bf[:, t * P:(t + 1) * P], cw_parts[:, t, :], ident_bf[:, :])
                last.then_inc(cw_turned, 1)

            def recur(m):
                yield M_TURN
                pe.wait_ge(y_out, m + 1)
                pe.wait_ge(x_ready, NBLK + m)
                turn(PS_A, lambda t: yT[:, t * P:(t + 1) * P]).then_inc(y_turned, 1)
                yield M_TURN_Z
                pe.wait_ge(rec_ln.z_ready, BT * (m + 1))
                turn(PS_A, lambda t: z[:, t, :]).then_inc(zm_turned, 1)
                yield M_EMB
                pe.wait_ge(zmT_ready, m + 1)
                pe.wait_ge(scores_ready, NBLK + m)
                nc.tensor.matmul(bank(PS_A), w_in[:, 0:D], zT[:, :], start=True, stop=True)
                nc.tensor.matmul(ps[0:SD, PS_B, :], w_in[:, D:D + SD], zT[:, :], start=True, stop=True).then_inc(emb_ps, 1)
                yield M_GATE
                pe.wait_ge(embT_ready, m + 1)
                pe.wait_ge(siT_ready, m + 1)
                nc.tensor.matmul(ps[0:SD, PS_A, :], w_g[:, :], embT, start=True, stop=False)
                nc.tensor.matmul(ps[0:SD, PS_A, :], w_g_s[:, :], siT, start=False, stop=True).then_inc(gate_ps, 1)
                yield M_MIX
                pe.wait_ge(scan_step, SCAN_STEPS * (m + 1))
                for t in range(BT):
                    cols = slice(t * P, (t + 1) * P)
                    nc.tensor.matmul(ps[:, PS_A, cols], embT[:, cols], w_out[:, :], start=True, stop=False)
                    last = nc.tensor.matmul(ps[:, PS_A, cols], stT[:, cols], w_out_s[:, :], start=False, stop=True)
                last.then_inc(mix_ready, 1)

            def output(o, unit=O_TURN):
                yield unit
                pe.wait_ge(y_out, NBLK + o + 1)
                if o:
                    pe.wait_ge(out_ready, o)
                else:
                    pe.wait_ge(x_ready, FFN_BLOCKS)
                turn(PS_A, lambda t: yT[:, t * P:(t + 1) * P]).then_inc(y_turned, 1)

            def times(dst, w, cols, hi, lo, start, stop):
                nc.tensor.matmul(dst, W_hi[w][:, cols], hi, start=start, stop=False)
                nc.tensor.matmul(dst, W_hi[w][:, cols], lo, start=False, stop=False)
                return nc.tensor.matmul(dst, W_lo[w][:, cols], hi, start=False, stop=stop)

            def down(u, seen):
                pe.wait_ge(lo_ready, seen)
                times(bank(PS_Y), 2, slice(u * P, (u + 1) * P), hid_hi[:, u % HBUF, :], hid_lo[:, u % HBUF, :],
                      u == 0, u == UNITS - 1).then_inc(down_done, 1)

            def ffn(p, slot, sides, first=False):
                blk = ds(slot * BLK, BLK)
                pe.wait_ge(xl_ready, p + 1)
                for u in range(UNITS):
                    cols = slice(u * P, (u + 1) * P)
                    if first and u % WCH == 0:
                        pe.wait_ge(piece_lo, 3 * (u // WCH + 1))
                    if not first or u >= 2:
                        pe.wait_ge(silu_ready, freed(p, u))
                    times(bank(PS_G[u % 2]), 0, cols, xh[:, blk], xl[:, blk], True, True).then_inc(g_ready, 1)
                    if u in HALF_AT:
                        half = HALF_AT.index(u)
                        if half == 0:
                            pe.wait_ge(routed, p + 1)
                        if half or not first:
                            pe.wait_ge(hid_ready, p * UNITS + u - 1 if half else p * UNITS - 1)
                        nc.tensor.matmul(bank(PS_C), expert_of[:, half * P:(half + 1) * P], cwT[:, blk],
                                         start=True, stop=True).then_inc(c_ready, 1)
                    if not first or u >= 2:
                        pe.wait_ge(*product_done(p, u))
                    times(bank(PS_U[u % 2]), 1, cols, xh[:, blk], xl[:, blk], True, True).then_inc(u_ready, 1)
                    if u == LAG and not first:
                        pe.wait_ge(y_out, p)
                    if u >= LAG or not first:
                        down((u - LAG) % UNITS, p * UNITS + u - LAG + 1)
                    beside(sides, u)

            pe.wait_ge(ident_ready, 2)
            attn_turn(0)
            attn_turn(1)
            pe.wait_ge(attn_loaded, 16 * len(ATTN_IN))
            for a in range(2):
                for t in range(BT):
                    attn_qkv(a, t)
                attn_kv(a)
            r0, b0, b1 = started(route(0, (den_ready, 2), first=True)), started(attend(0, yT)), started(attend(1, yT))
            beside([b0], B_NUM)
            attn_turn(2)
            attn_qkv(2, 0)
            attn_qkv(2, 1)
            beside([b0], B_TURN)
            attn_qkv(2, 2)
            attn_qkv(2, 3)
            beside([b0], B_PROJ)
            attn_kv(2)
            attn_turn(3)
            beside([r0], R_TURN)
            attn_qkv(3, 0)
            attn_qkv(3, 1)
            pe.wait_ge(const_loaded, 16 * len(CONST_IN))
            beside([r0], R_LOGIT)
            attn_qkv(3, 2)
            attn_qkv(3, 3)
            attn_kv(3)
            beside([b1], B_TURN)
            beside([r0], R_TURN_CW)
            beside([b1], B_PROJ)
            ffn(0, 0, [started(route(1, (den_ready, 3))), started(attend(attn_block(0), zT))], first=True)
            ffn(1, 1, [started(route(2, (den_ready, 4))), started(attend(attn_block(1), zT))])
            with pe.Fori(2, LAST_REC + 1) as p:
                ffn(p, p % NBLK, [started(route(p + 1, (siT_ready, p - 1))), started(recur(p - 2))])
            ffn(FFN_BLOCKS - 2, NBLK - 2, [started(route(FFN_BLOCKS - 1)), started(output(0))])
            ffn(FFN_BLOCKS - 1, NBLK - 1, [started(output(1)), started(output(2, O_TURN2))])
            for u in range(UNITS - LAG, UNITS):
                down(u, (FFN_BLOCKS - 1) * UNITS + u + 1)
            beside([started(output(3))], O_TURN)


def kernel(**inputs):
    import numpy as np
    import ml_dtypes
    import concourse.bacc as _bacc
    from concourse import mybir as _mybir
    from concourse.bass_utils import run_bass_kernel_spmd as _run

    g = {k: np.asarray(v) for k, v in inputs.items()}
    order = np.concatenate([np.arange(0, D, 2), np.arange(1, D, 2)])

    def units(routed, shared):
        halves = routed.reshape(HALVES, EH, HU, BAND, D).transpose(0, 2, 1, 3, 4).reshape(HALVES, HU * P, D)
        full = np.zeros((HID, D), np.float32)
        for half in range(HALVES):
            at = HALF_AT[half] * P
            full[at:at + HU * P] = halves[half]
        for i, u in enumerate(SHARED_AT):
            rows = shared[i * P:(i + 1) * P]
            full[u * P:u * P + rows.shape[0]] = rows
        return full

    gate = units(g["L0_ffn_gate_proj"], g["L0_ffn_shared_gate_w"]).T
    up = units(g["L0_ffn_up_proj"], g["L0_ffn_shared_up_w"]).T
    down = units(g["L0_ffn_down_proj"].transpose(0, 2, 1), g["L0_ffn_shared_down_w"].T)
    down = down.reshape(UNITS, P, D).transpose(1, 0, 2).reshape(P, HID)

    freqs = np.float32(1.0) / np.float32(10000.0) ** (np.arange(0, HD, 2, dtype=np.float32) / np.float32(HD))
    ang = (np.arange(SEQ, dtype=np.float32)[:, None] * freqs[None, :]).astype(np.float32)
    cos = np.tile(np.cos(ang).astype(np.float32), (1, HEADS)).reshape(SEQ // P, P, D // 2).transpose(1, 0, 2)
    sin = np.tile(np.sin(ang).astype(np.float32), (1, HEADS)).reshape(SEQ // P, P, D // 2).transpose(1, 0, 2)
    head = np.arange(D // 2) // (HD // 2)
    head = np.concatenate([head, head])
    value_head = np.concatenate([np.arange(D) // HD, np.arange(HEADS)])
    expert_of = np.zeros((P, HALVES * P), np.float32)
    for part in range(PARTS):
        expert_of[part * E + np.arange(HALVES * P) // BAND, np.arange(HALVES * P)] = 1.0
    rows = {
        "x": g["L0_attn_a_x"].reshape(BATCH * SEQ, D),
        "w_qkv": np.concatenate([g["L0_attn_a_Wq"][:, order], g["L0_attn_a_Wk"][:, order], g["L0_attn_a_Wv"]], axis=1),
        "w_o": g["L0_attn_a_Wo"],
        "head_mask": (head[:, None] == value_head[None, :]).astype(np.float32),
        "cos": cos,
        "sin": np.stack([sin, -sin], axis=2),
        "w_route": g["L0_ffn_gate_w"].T,
        "bias_route": np.repeat(g["L0_ffn_gate_bias"][None, :], P, axis=0),
        "tile_inner": np.repeat((np.arange(BT * E) % E != 0).astype(np.float32)[None, :], P, axis=0),
        "thr_g": np.repeat(np.arange(GROUPS, dtype=np.float32)[None, :] - (GROUPS - 1 - TOPG), P, axis=0),
        "lower_g": np.repeat(np.tril(np.ones((GROUPS, GROUPS), np.float32), -1)[None], P, axis=0),
        "b_in": g["L0_attn_b_b_in"][:D, None],
        "b_in_s": g["L0_attn_b_b_in"][D:, None],
        "w_in": g["L0_attn_b_W_in"],
        "w_g": g["L0_attn_b_W_g"][:D],
        "w_g_s": g["L0_attn_b_W_g"][D:],
        "b_g": g["L0_attn_b_b_g"][:, None],
        "w_out": g["L0_attn_b_W_out"][:D],
        "w_out_s": np.concatenate([g["L0_attn_b_W_out"][D:], g["L0_attn_b_b_out"][None, :]], axis=0),
        "keep": np.repeat((np.arange(1, NBLK + 1) % (SEQ // BLK) != 0).astype(np.float32)[None, :], SD, axis=0),
        "expert_of": expert_of.astype(ml_dtypes.bfloat16),
        "gate_proj": gate,
        "up_proj": up,
        "down_proj": down,
    }
    nc = _bacc.Bacc("TRN2", target_bir_lowering=False, num_devices=1)
    arrays, args = {}, {}
    for name, a in rows.items():
        a = np.ascontiguousarray(a)
        arrays[f"{name}_dram"] = a
        args[name] = nc.dram_tensor(f"{name}_dram", a.shape, _mybir.dt.from_np(a.dtype), kind="ExternalInput").ap()
    out = nc.dram_tensor("out_dram", (BATCH * SEQ, D), _mybir.dt.float32, kind="ExternalOutput").ap()
    hybrid_kernel(nc, args, out)
    r = _run(nc, [arrays], core_ids=[0])
    return r.results[0]["out_dram"].reshape(BATCH, SEQ, D)
```

```python
import concourse.bass as bass
from concourse import mybir
from contextlib import ExitStack

P = 128
BATCH, SEQ, D = 2, 1024, 128
TILES = BATCH * SEQ // P
BT = 4
BLK = BT * P
NBLK = TILES // BT
HEADS, HD = 16, 8
E, I, NS = 16, 176, 2
GROUPS, TOPG, TOPK = 4, 2, 4
GE = E // GROUPS
HALVES = 2
EH = E // HALVES
BAND = P // EH
HU = I // BAND
EU = HALVES * HU
SHARED = I * NS
UNITS = EU + -(-SHARED // P)
HID = UNITS * P
SHARED_AT = (0, HU + 1, 2 * HU + 2)
HALF_AT = (1, HU + 2)
SD = 8
GATE_AT = 32
SMALL = GATE_AT + SD
KVW = D + HEADS
LN_EPS, DEN_EPS, TOPK_EPS, TINY = 1e-5, 1e-6, 1e-20, 1e-20
PARTS = 3
WCH = 5
PIECES = UNITS // WCH
RING = 3

EARLY = 6
LAG = 3
HBUF = 5

R_STATS, R_MV, R_POW, R_Z, R_TURN, R_OUT, R_LO, R_LOGIT, R_GUARD, R_SCORE = 0, 1, 1, 3, 5, 6, 6, 7, 7, 7
R_RANK, R_TURN_CW, R_CW_OUT = (8, 9, 10, 12, 13, 14, 15, 16, 17, 19), 21, 22
B_NUM, B_DEN, B_TURN, B_OUT, B_PROJ, B_SUM = 9, 10, 12, 13, 14, 15
M_TURN, M_SUM, M_STATS, M_MV, M_POW, M_Z, M_TURN_Z, M_OUT = 1, 2, 4, 5, 6, 8, 11, 12
M_GATE, M_SIG, M_SCAN, M_MIX, M_X = 13, 14, (15, 18, 20), 21, 22
F_FOLD, F_OUT = 17, 18
Y_OUT = LAG - 1
O_TURN, O_SUM, O_TURN2, O_SUM2 = 0, 1, 6, 7


def hybrid_kernel(nc, A, out):
    f32, f32r, bf16 = mybir.dt.float32, mybir.dt.float32r, mybir.dt.bfloat16
    ALU, ACT, AX = mybir.AluOpType, mybir.ActivationFunctionType, mybir.AxisListType
    ds = bass.ds
    ctx = ExitStack()
    with ctx:
        def sb(name, shape, dt=f32):
            return ctx.enter_context(nc.sbuf_tensor(name, shape, dt))

        def sem(name):
            return ctx.enter_context(nc.semaphore(name))

        W_hi = [sb(f"{n}_hi", [P, HID], f32r) for n in ("gate_proj", "up_proj", "down_proj")]
        W_lo = [sb(f"{n}_lo", [P, HID], f32r) for n in ("gate_proj", "up_proj", "down_proj")]
        stage = sb("stage", [P, RING, WCH * P])
        xh = sb("xh", [P, NBLK * BLK], f32r)
        xl = sb("xl", [P, NBLK * BLK], f32r)
        cwT = sb("cwT", [P, NBLK * BLK], bf16)
        expert_of = sb("expert_of", [P, HALVES * P], bf16)
        x_tok = sb("x_tok", [P, TILES, D])
        silu_sb = sb("silu_sb", [P, 2, BLK])
        act_sb = sb("act_sb", [P, 2, BLK])
        hid_sb = sb("hid_sb", [P, 2, BLK])
        hid_hi = sb("hid_hi", [P, HBUF, BLK], f32r)
        hid_lo = sb("hid_lo", [P, HBUF, BLK], f32r)
        w_qkv = sb("w_qkv", [P, 3 * D])
        w_o = sb("w_o", [P, D])
        cos_t = sb("cos_t", [P, SEQ // P, D // 2])
        sin_t = sb("sin_t", [P, SEQ // P, 2, D // 2])
        head_mask = sb("head_mask", [P, KVW])
        rot_a = sb("rot_a", [P, 2, 2, 2, D // 2])
        rot_b = sb("rot_b", [P, 2, 2, 2, D // 2])
        rot = sb("rot", [P, 2, 2, 2, D // 2])
        qk = sb("qk", [P, BT, 2, D])
        v_pad = sb("v_pad", [P, BT, KVW])
        qk_of = (qk, act_sb[:, :, :].rearrange("p a b -> p (a b)").rearrange("p (t a d) -> p t a d", t=BT, a=2))
        v_of = (v_pad, silu_sb[:, :, :].rearrange("p a b -> p (a b)")[:, 0:BT * KVW].rearrange("p (t e) -> p t e", t=BT))
        qT = sb("qT", [P, NBLK * BLK])
        kv_half = sb("kv_half", [P, KVW])
        kv_sum = sb("kv_sum", [P, KVW])
        kv = sb("kv", [P, BATCH, KVW])
        den = sb("den", [P, BT * HEADS])
        rden = sb("rden", [P, BT * HEADS])
        xcur = sb("xcur", [P, BT, D])
        z = sb("z", [P, BT, D])
        zT = sb("zT", [P, BLK])
        yT = sb("yT", [P, BLK])
        zr = sb("zr", [P, BT, D])
        zrT = sb("zrT", [P, BLK])
        w_inT = sb("w_inT", [P, D])
        w_inT_s = sb("w_inT_s", [SD, D])
        w_in_s = sb("w_in_s", [P, SMALL])
        b_in = sb("b_in", [P, SD + 1])
        b_in_s = sb("b_in_s", [SD, 1])
        w_g = sb("w_g", [P, SMALL])
        w_g_s = sb("w_g_s", [SD, SMALL])
        b_small_in = sb("b_small_in", [SMALL, 1])
        w_out = sb("w_out", [P, D])
        w_out_s = sb("w_out_s", [SD + 1, D])
        w_mix = sb("w_mix", [P, D])
        w_mix_s = sb("w_mix_s", [SD + 1, D])
        w_small = sb("w_small", [P, SMALL])
        b_small = sb("b_small", [SMALL, 1])
        b_half = sb("b_half", [SMALL, 1])
        thT = rot_a[0:SD].rearrange("p t a b d -> p (t a b d)")
        gT = rot_b[0:SD].rearrange("p t a b d -> p (t a b d)")
        omgT = rot[0:SD].rearrange("p t a b d -> p (t a b d)")
        inT = qT[0:SD, 0:BLK]
        stT = sb("stT", [SD + 1, BLK])
        carry = sb("carry", [SD, 1])
        keep = sb("keep", [SD, NBLK])
        rec_shift = sb("rec_shift", [P, BT])
        w_route = sb("w_route", [P, E])
        bias_route = sb("bias_route", [P, E])
        lower_g = sb("lower_g", [P, GROUPS, GROUPS])
        tile_inner = sb("tile_inner", [P, BT * E])
        thr_g = sb("thr_g", [P, GROUPS])
        logit = sb("logit", [P, 4, BT * E])
        positive = sb("positive", [P, BT * E])
        half_sig = sb("half_sig", [P, 2, BT * E])
        silu_logit = sb("silu_logit", [P, BT * E])
        scores = sb("scores", [P, BT, E])
        sfc = sb("sfc", [P, BT, E])
        pair_hi = sb("pair_hi", [P, BT * E // 2])
        pair_lo = sb("pair_lo", [P, BT * E // 2])
        quad = sb("quad", [P, 5, BT * GROUPS])
        beats_g = sb("beats_g", [P, BT, GROUPS, GROUPS])
        rank_g = sb("rank_g", [P, 4, BT * GROUPS])
        masked = sb("masked", [P, BT, E])
        best = sb("best", [P, BT, 8])
        above = sb("above", [P, BT, E])
        level = sb("level", [P, BT, E])
        tied = sb("tied", [P, 4, BT * E])
        chosen = sb("chosen", [P, BT * E])
        wsum = sb("wsum", [P, 4, BT])
        cw = sb("cw", [P, BT, E])
        cw_left = sb("cw_left", [P, 2, BT, E])
        cw_parts = sb("cw_parts", [P, BT, P], bf16)
        ident = sb("ident", [P, P])
        ident_bf = sb("ident_bf", [P, P], bf16)
        neg_half = sb("neg_half", [P, BT])

        class Norm:
            def __init__(self, name, n):
                self.n = n
                self.stats = sb(f"{name}_stats", [P, n, 6])
                self.mv = sb(f"{name}_mv", [P, 5, n])
                self.neg_mean = sb(f"{name}_neg_mean", [P, n])
                self.vpe = sb(f"{name}_vpe", [P, n])
                self.rstd = sb(f"{name}_rstd", [P, n])
                self.stats_ready, self.mv_ready = sem(f"{name}_stats_ready"), sem(f"{name}_mv_ready")
                self.vpe_ready, self.rstd_ready = sem(f"{name}_vpe_ready"), sem(f"{name}_rstd_ready")
                self.z_ready = sem(f"{name}_z_ready")

        attn_ln, route_ln, rec_ln = Norm("attn", BT), Norm("route", BT), Norm("rec", BT)

        ps = ctx.enter_context(nc.psum_tensor("ps", [P, 8, BLK], f32))
        PS_G, PS_U, PS_C, PS_Y, PS_A, PS_B = (0, 1), (2, 3), 4, 5, 6, 7

        def bank(b):
            return ps[:, b, :]

        def tiles(b):
            return ps[:, b, :].rearrange("p (t d) -> p t d", t=BT)

        fold_mix, fold_mix_s = ps[:, PS_A, 0:D], ps[0:SD + 1, PS_A, D:2 * D]
        fold_small, fold_bias = ps[:, PS_A, 2 * D:2 * D + SMALL], ps[0:SMALL, PS_A, 3 * D:3 * D + 1]
        psB_bf = ps[:, PS_B, 0:BLK // 2].bitcast(bf16)

        x_loaded = [sem(f"x_loaded{b}") for b in range(NBLK)]
        attn_loaded, const_loaded = sem("attn_loaded"), sem("const_loaded")
        piece_loaded = [sem(f"piece_loaded{i}") for i in range(RING)]
        piece_hi, piece_lo = sem("piece_hi"), sem("piece_lo")
        ident_zero, ident_ready = sem("ident_zero"), sem("ident_ready")
        z_turned, zT_ready, qkv_ready, rot_mul = sem("z_turned"), sem("zT_ready"), sem("qkv_ready"), sem("rot_mul")
        rot_ready, v_ready, qk_ready, q_turned = sem("rot_ready"), sem("v_ready"), sem("qk_ready"), sem("q_turned")
        kv_multiplied = sem("kv_multiplied")
        qT_ready, kv_out, kv_summed, kv_ready = sem("qT_ready"), sem("kv_out"), sem("kv_summed"), sem("kv_ready")
        num_ready, den_ready, rden_ready, att_ready = sem("num_ready"), sem("den_ready"), sem("rden_ready"), sem("att_ready")
        att_turned, attT_ready, proj_ready, x_ready = sem("att_turned"), sem("attT_ready"), sem("proj_ready"), sem("x_ready")
        zr_turned, zrT_ready, xh_ready, xl_ready = sem("zr_turned"), sem("zrT_ready"), sem("xh_ready"), sem("xl_ready")
        logits_ready, logit_out, scores_ready = sem("logits_ready"), sem("logit_out"), sem("scores_ready")
        route_step = sem("route_step")
        cw_split, cw_turned, routed = sem("cw_split"), sem("cw_turned"), sem("routed")
        g_ready, u_ready, c_ready = sem("g_ready"), sem("u_ready"), sem("c_ready")
        silu_ready, act_ready, hid_ready = sem("silu_ready"), sem("act_ready"), sem("hid_ready")
        hi_ready, lo_ready, down_done, y_out = sem("hi_ready"), sem("lo_ready"), sem("down_done"), sem("y_out")
        y_turned, xcur_ready, zm_turned, zmT_ready = sem("y_turned"), sem("xcur_ready"), sem("zm_turned"), sem("zmT_ready")
        fold_ps, folded, shift_ready = sem("fold_ps"), sem("folded"), sem("shift_ready")
        gate_ps, thT_ready, scan_step, mix_ready = sem("gate_ps"), sem("thT_ready"), sem("scan_step"), sem("mix_ready")
        out_ready, out_stored = sem("out_ready"), sem("out_stored")

        block = ctx.enter_context(nc.Block())

        ATTN_IN = ("w_qkv", "w_o", "head_mask", "cos", "sin")
        CONST_IN = ("w_route", "bias_route", "tile_inner", "thr_g", "lower_g", "expert_of", "w_inT",
                    "w_inT_s", "w_in_s", "b_in", "b_in_s", "w_g", "w_g_s", "b_small_in", "w_out", "w_out_s", "keep")
        place = {"w_qkv": w_qkv, "w_o": w_o, "head_mask": head_mask, "cos": cos_t, "sin": sin_t, "w_route": w_route,
                 "bias_route": bias_route, "tile_inner": tile_inner, "thr_g": thr_g, "lower_g": lower_g,
                 "expert_of": expert_of, "w_inT": w_inT, "w_inT_s": w_inT_s, "w_in_s": w_in_s, "b_in": b_in,
                 "b_in_s": b_in_s, "w_g": w_g, "w_g_s": w_g_s, "b_small_in": b_small_in, "w_out": w_out, "w_out_s": w_out_s, "keep": keep}
        LOGIT_STEPS, ROUTE_STEPS, CW_SPLITS, MV_STEPS, SCAN_STEPS, FOLDED = 5, 35, 2 * PARTS - 1, 6, 5, 5
        FFN_BLOCKS = 2 * NBLK
        LAST_REC = NBLK + 1
        a_z, a_zT, a_bank = (z, zr, z, z), (zT, zrT, zT, yT), (0, 1, 0, 1)
        qkv_banks, q_bank, kv_bank = ((2, 3, 6, 7), (2, 3, 6, 7), (2, 3, 0, 2), (3, 0, 2, 3)), 4, 5

        def started(steps):
            return [steps, next(steps)]

        def beside(sides, u):
            for side in sides:
                while side[1] <= u:
                    side[1] = next(side[0], 2 * UNITS)

        def freed(p, u):
            return p * UNITS + u - 1 if u >= 2 else p * UNITS - u

        def product_done(p, u):
            w, through = (u - 2, p) if u >= 2 else (UNITS - 1 - u, p - 1)
            if w in SHARED_AT:
                return hid_ready, through * UNITS + w + 1
            return act_ready, through * EU + routed_units(w) + 1

        def routed_units(u):
            return u - sum(s < u for s in SHARED_AT)

        def last_step(side):
            yield 0
            beside([side], UNITS)

        def pieces(split):
            for n in range(EARLY, 3 * PIECES):
                yield 2 * (n - EARLY)
                split(n)

        def attn_block(p):
            return p + 2

        def weight_piece(n):
            w, c = n % 3, n // 3
            return w, slice(c * WCH * P, (c + 1) * WCH * P)

        @block.sync
        def _(sp):
            x_in = A["x"].rearrange("(b t p) d -> b p t d", p=P, t=BT)
            for b in range(NBLK):
                if b == BATCH:
                    for name in ATTN_IN:
                        sp.dma_start(place[name][:], A[name]).then_inc(attn_loaded, 16)
                sp.dma_start(x_tok[:, b * BT:(b + 1) * BT, :], x_in[b]).then_inc(x_loaded[b], 16)
            for n in range(3 * PIECES):
                if n == RING:
                    for name in CONST_IN:
                        sp.dma_start(place[name][:], A[name]).then_inc(const_loaded, 16)
                if n >= RING:
                    sp.wait_ge(piece_lo, n - RING + 1)
                w, cols = weight_piece(n)
                sp.dma_start(stage[:, n % RING, :], A[("gate_proj", "up_proj", "down_proj")[w]][:, cols])\
                    .then_inc(piece_loaded[n % RING], 16)
            for o in range(NBLK):
                sp.wait_ge(out_ready, o + 1)
                sp.dma_start(out.rearrange("(b t p) d -> b p t d", p=P, t=BT)[o], xcur[:, :, :]).then_inc(out_stored, 16)
            sp.wait_ge(out_stored, 16 * NBLK)

        @block.gpsimd
        def _(pool):
            nc.gpsimd.memset(ident[:, :], 0.0).then_inc(ident_zero, 1)
            nc.gpsimd.memset(neg_half[:, :], -0.5)
            for v in v_of:
                nc.gpsimd.memset(v[:, :, :], 1.0)
            nc.gpsimd.memset(cw_parts[:, :, :], 0.0)
            nc.gpsimd.memset(stT[:, :], 1.0)
            nc.gpsimd.memset(carry[:, :], 0.0)
            pool.wait_ge(ident_zero, 1)
            nc.gpsimd.affine_select(out=ident[:, :], in_=ident[:, :], compare_op=ALU.not_equal, fill=1.0,
                                    base=0, pattern=[[-1, P]], channel_multiplier=1).then_inc(ident_ready, 1)

            def rstd(ln, k):
                pool.wait_ge(ln.vpe_ready, k + 1)
                nc.gpsimd.tensor_tensor(ln.rstd[:, :], ln.vpe[:, :], neg_half[:, :], ALU.pow).then_inc(ln.rstd_ready, 1)

            def rotate(a, t):
                n = a * BT + t
                pool.wait_ge(rot_mul, 2 * n + 2)
                if n >= 2:
                    pool.wait_ge(qk_ready, n - 1)
                nc.gpsimd.tensor_tensor(rot[:, t % 2, :, 0, :], rot_a[:, t % 2, :, 0, :],
                                        rot_b[:, t % 2, :, 1, :], ALU.add)
                nc.gpsimd.tensor_tensor(rot[:, t % 2, :, 1, :], rot_a[:, t % 2, :, 1, :],
                                        rot_b[:, t % 2, :, 0, :], ALU.add).then_inc(rot_ready, 1)

            def weight_lo(n):
                w, cols = weight_piece(n)
                pool.wait_ge(piece_hi, n + 1)
                nc.gpsimd.tensor_tensor(W_lo[w][:, cols], stage[:, n % RING, :], W_hi[w][:, cols].bitcast(f32),
                                        ALU.subtract).then_inc(piece_lo, 1)

            def route(r, slot):
                yield R_POW
                rstd(route_ln, r)
                yield R_LO
                pool.wait_ge(xh_ready, r + 1)
                nc.gpsimd.tensor_tensor(xl[:, ds(slot * BLK, BLK)], zrT[:, :],
                                        xh[:, ds(slot * BLK, BLK)].bitcast(f32), ALU.subtract).then_inc(xl_ready, 1)

            def recur(m):
                yield M_POW
                rstd(rec_ln, m)
                pool.wait_ge(rec_ln.rstd_ready, m + 1)
                nc.gpsimd.tensor_tensor(rec_shift[:, :], rec_ln.neg_mean[:, :], rec_ln.rstd[:, :], ALU.mult)\
                    .then_inc(shift_ready, 1)

            def ffn(p, sides):
                for u in range(UNITS):
                    pool.wait_ge(hi_ready, p * UNITS + u + 1)
                    nc.gpsimd.tensor_tensor(hid_lo[:, u % HBUF, :], hid_sb[:, u % 2, :],
                                            hid_hi[:, u % HBUF, :].bitcast(f32), ALU.subtract).then_inc(lo_ready, 1)
                    beside(sides, u)

            pool.wait_ge(ident_ready, 1)
            rstd(attn_ln, 0)
            rstd(attn_ln, 1)
            for a in range(2):
                for t in range(BT):
                    rotate(a, t)
            rstd(attn_ln, 2)
            r0 = started(route(0, 0))
            weight_lo(0)
            weight_lo(1)
            rstd(attn_ln, 3)
            rotate(2, 0)
            weight_lo(2)
            beside([r0], R_POW)
            weight_lo(3)
            for t in range(1, BT):
                rotate(2, t)
            beside([r0], R_LO)
            weight_lo(4)
            rotate(3, 0)
            weight_lo(5)
            rotate(3, 1)
            rotate(3, 2)
            rotate(3, 3)
            ffn(0, [started(pieces(weight_lo)), started(route(1, 1))])
            ffn(1, [started(route(2, 2))])
            with pool.Fori(2, LAST_REC + 1) as p:
                ffn(p, [started(route(p + 1, (p + 1) % NBLK)), started(recur(p - 2))])
            ffn(FFN_BLOCKS - 2, [started(route(FFN_BLOCKS - 1, NBLK - 1))])
            ffn(FFN_BLOCKS - 1, [])

        @block.scalar
        def _(act):
            def turned(a):
                act.wait_ge(z_turned, a + 1)
                nc.scalar.activation(a_zT[a][:, :], bank(a_bank[a]), ACT.Copy).then_inc(zT_ready, 1)

            def values(a, t):
                n = a * BT + t
                src = bank(qkv_banks[a][t])
                if a >= 2 and t == 0:
                    act.wait_ge(q_turned, a - 1)
                act.wait_ge(rot_mul, 2 * n + 2)
                nc.scalar.activation(v_of[a % 2][:, t, 0:D], src[:, 2 * D:3 * D], ACT.Copy).then_inc(v_ready, 1)
                act.wait_ge(rot_ready, n + 1)
                nc.scalar.activation(qk_of[a % 2][:, t, :, :], rot[:, t % 2, :, :, :].rearrange("p a b d -> p a (b d)"),
                                     ACT.Relu).then_inc(qk_ready, 1)

            def queries(a):
                act.wait_ge(q_turned, a + 1)
                nc.scalar.activation(qT[:, a * BLK:(a + 1) * BLK], bank(q_bank), ACT.Copy).then_inc(qT_ready, 1)

            def weight_hi(n):
                w, cols = weight_piece(n)
                act.wait_ge(piece_loaded[n % RING], 16 * (n // RING + 1))
                nc.scalar.activation(W_hi[w][:, cols], stage[:, n % RING, :], ACT.Copy).then_inc(piece_hi, 1)

            def attend(b, attT):
                yield B_OUT
                act.wait_ge(att_turned, b + 1)
                nc.scalar.activation(attT[:, :], bank(PS_A), ACT.Copy).then_inc(attT_ready, 1)

            def route(r, slot, cw_out_at=R_CW_OUT):
                yield R_OUT
                act.wait_ge(zr_turned, r + 1)
                nc.scalar.activation(zrT[:, :], bank(PS_B), ACT.Copy).then_inc(zrT_ready, 1)
                nc.scalar.activation(xh[:, ds(slot * BLK, BLK)], bank(PS_B), ACT.Copy).then_inc(xh_ready, 1)
                yield R_SCORE
                act.wait_ge(logit_out, LOGIT_STEPS * (r + 1))
                nc.scalar.activation(silu_logit[:, :], logit[:, 1, :], ACT.Silu).then_inc(scores_ready, 1)
                yield cw_out_at
                act.wait_ge(cw_turned, r + 1)
                act.wait_ge(xl_ready, r + 1)
                nc.scalar.activation(cwT[:, ds(slot * BLK, BLK)], psB_bf, ACT.Copy).then_inc(routed, 1)

            def y_copy(p, turned_before):
                act.wait_ge(down_done, p * UNITS)
                if turned_before:
                    act.wait_ge(y_turned, p - 1)
                nc.scalar.activation(yT[:, :], bank(PS_Y), ACT.Copy).then_inc(y_out, 1)

            def leave(p, turned_before=True):
                yield Y_OUT
                y_copy(p, turned_before)

            def recur(m):
                yield M_Z
                act.wait_ge(shift_ready, m + 1)
                for t in range(BT):
                    if t == BT // 2:
                        yield M_Z + 1
                    nc.scalar.activation(z[:, t, :], xcur[:, t, :], ACT.Identity, bias=rec_shift[:, t:t + 1],
                                         scale=rec_ln.rstd[:, t:t + 1]).then_inc(rec_ln.z_ready, 1)
                yield M_OUT
                act.wait_ge(zm_turned, m + 1)
                nc.scalar.activation(zT[:, :], bank(PS_A), ACT.Copy).then_inc(zmT_ready, 1)
                yield M_SIG
                act.wait_ge(gate_ps, m + 1)
                nc.scalar.activation(thT, ps[GATE_AT:SMALL, PS_A, :], ACT.Tanh,
                                     bias=b_half[GATE_AT:SMALL, 0:1], scale=0.5).then_inc(thT_ready, 1)

            def hid_high(p, u, first):
                act.wait_ge(hid_ready, p * UNITS + u + 1)
                if not first or u >= HBUF:
                    act.wait_ge(down_done, p * UNITS + u + 1 - HBUF)
                nc.scalar.activation(hid_hi[:, u % HBUF, :], hid_sb[:, u % 2, :], ACT.Copy).then_inc(hi_ready, 1)

            def ffn(p, sides, first=False):
                for u in range(UNITS):
                    act.wait_ge(g_ready, p * UNITS + u + 1)
                    if not first or u >= 2:
                        act.wait_ge(*product_done(p, u))
                    nc.scalar.activation(silu_sb[:, u % 2, :], bank(PS_G[u % 2]), ACT.Silu).then_inc(silu_ready, 1)
                    if u >= 1:
                        hid_high(p, u - 1, first)
                    beside(sides, u)
                hid_high(p, UNITS - 1, first)

            act.wait_ge(ident_ready, 1)
            nc.scalar.activation(ident_bf[:, :], ident[:, :], ACT.Copy).then_inc(ident_ready, 1)
            turned(0)
            values(0, 0)
            turned(1)
            for t in range(1, BT):
                values(0, t)
            for t in range(BT - 1):
                values(1, t)
            queries(0)
            values(1, BT - 1)
            queries(1)
            r0, b0, b1 = started(route(0, 0, UNITS)), started(attend(0, yT)), started(attend(1, zT))
            weight_hi(0)
            weight_hi(1)
            turned(2)
            beside([b0], B_OUT)
            weight_hi(2)
            values(2, 0)
            weight_hi(3)
            weight_hi(4)
            turned(3)
            beside([r0], R_OUT)
            for t in range(1, BT):
                values(2, t)
            beside([r0], R_SCORE)
            weight_hi(5)
            values(3, 0)
            values(3, 1)
            queries(2)
            values(3, 2)
            beside([b1], B_OUT)
            values(3, 3)
            queries(3)
            ffn(0, [started(last_step(r0)), started(pieces(weight_hi)), started(route(1, 1)), started(attend(attn_block(0), zT))], first=True)
            ffn(1, [started(leave(1, False)), started(route(2, 2)), started(attend(attn_block(1), zT))])
            act.wait_ge(folded, FOLDED)
            with act.Fori(2, LAST_REC + 1) as p:
                ffn(p, [started(leave(p)), started(route(p + 1, (p + 1) % NBLK)), started(recur(p - 2))])
            ffn(FFN_BLOCKS - 2, [started(leave(FFN_BLOCKS - 2)), started(route(FFN_BLOCKS - 1, NBLK - 1))])
            ffn(FFN_BLOCKS - 1, [started(leave(FFN_BLOCKS - 1))])
            y_copy(FFN_BLOCKS, True)

        @block.vector
        def _(dve):
            def norm_stats(ln, src):
                for t in range(ln.n):
                    nc.vector.bn_stats(ln.stats[:, t, :], src(t)).then_inc(ln.stats_ready, 1)

            def norm_mv(ln, k):
                stats, mv = ln.stats, ln.mv
                dve.wait_ge(ln.stats_ready, ln.n * k + ln.n)
                nc.vector.tensor_tensor(mv[:, 0, :], stats[:, :, 1], stats[:, :, 4], ALU.add).then_inc(ln.mv_ready, 1)
                nc.vector.tensor_tensor(mv[:, 1, :], stats[:, :, 1], stats[:, :, 4], ALU.subtract).then_inc(ln.mv_ready, 1)
                nc.vector.tensor_tensor(mv[:, 2, :], stats[:, :, 2], stats[:, :, 5], ALU.add).then_inc(ln.mv_ready, 1)
                dve.wait_ge(ln.mv_ready, MV_STEPS * k + 3)
                nc.vector.scalar_tensor_tensor(out=mv[:, 3, :], in0=mv[:, 1, :], scalar=0.25, in1=mv[:, 1, :],
                                               op0=ALU.mult, op1=ALU.mult).then_inc(ln.mv_ready, 1)
                nc.vector.tensor_scalar(mv[:, 4, :], mv[:, 2, :], 1.0 / D, LN_EPS, ALU.mult, ALU.add).then_inc(ln.mv_ready, 1)
                nc.vector.tensor_scalar(ln.neg_mean[:, :], mv[:, 0, :], -0.5, None, ALU.mult).then_inc(ln.mv_ready, 1)
                dve.wait_ge(ln.mv_ready, MV_STEPS * k + 6)
                nc.vector.tensor_tensor(ln.vpe[:, :], mv[:, 3, :], mv[:, 4, :], ALU.add).then_inc(ln.vpe_ready, 1)

            def norm(ln, k, dst, src, which=range(BT)):
                dve.wait_ge(ln.rstd_ready, k + 1)
                for t in which:
                    nc.vector.tensor_scalar(dst[:, t, :], src(t), ln.neg_mean[:, t:t + 1],
                                            ln.rstd[:, t:t + 1], ALU.add, ALU.mult).then_inc(ln.z_ready, 1)

            def tile_of(b):
                def src(t):
                    return x_tok[:, ds(b * BT + t, 1), :].rearrange("p t d -> p (t d)")
                return src

            def attn_stats(a):
                dve.wait_ge(x_loaded[a], 16)
                norm_stats(attn_ln, lambda t: x_tok[:, a * BT + t, :])
                norm_mv(attn_ln, a)

            def attn_norm(a):
                if a >= 2:
                    dve.wait_ge(z_turned, a if a == 3 else 1)
                norm(attn_ln, a, a_z[a], lambda t: x_tok[:, a * BT + t, :])

            def rotate(a, t):
                n, pos = a * BT + t, a % 2 * BT + t
                pst = ps[:, qkv_banks[a][t], 0:2 * D].rearrange("p (a b d) -> p a b d", a=2, b=2)
                dve.wait_ge(qkv_ready, n + 1)
                if n >= 2:
                    dve.wait_ge(rot_ready, n - 1)
                nc.vector.tensor_tensor(
                    rot_a[:, t % 2].rearrange("p a b d -> p (a b) d"), pst.rearrange("p a b d -> p (a b) d"),
                    cos_t[:, pos:pos + 1, :].to_broadcast([P, 4, D // 2]), ALU.mult).then_inc(rot_mul, 1)
                nc.vector.tensor_tensor(
                    rot_b[:, t % 2], pst,
                    sin_t[:, pos:pos + 1, :, :].to_broadcast([P, 2, 2, D // 2]), ALU.mult).then_inc(rot_mul, 1)

            def sum_kv(a):
                dve.wait_ge(kv_multiplied, a + 1)
                if a % 2 == 0:
                    nc.vector.tensor_copy(kv_half[:, :], ps[:, kv_bank, 0:KVW]).then_inc(kv_out, 1)
                else:
                    i = a // 2
                    dve.wait_ge(kv_out, 2 * i + 1)
                    nc.vector.tensor_tensor(kv_sum[:, :], ps[:, kv_bank, 0:KVW], kv_half[:, :], ALU.add).then_inc(kv_out, 1)
                    dve.wait_ge(kv_out, 2 * i + 2)
                    nc.vector.tensor_tensor(kv[:, i, :], kv_sum[:, :], head_mask[:, :], ALU.mult).then_inc(kv_ready, 1)

            def attend(b):
                yield B_DEN
                dve.wait_ge(num_ready, b + 1)
                nc.vector.tensor_scalar(den[:, :], ps[:, PS_B, 0:BT * HEADS], DEN_EPS, None, ALU.add).then_inc(den_ready, 1)
                dve.wait_ge(den_ready, b + 1)
                nc.vector.reciprocal(rden[:, :], den[:, :]).then_inc(rden_ready, 1)
                dve.wait_ge(rden_ready, b + 1)
                nc.vector.tensor_tensor(xcur[:, :, :].rearrange("p t (h e) -> p (t h) e", h=HEADS),
                                        bank(PS_A).rearrange("p (h e) -> p h e", e=HD),
                                        rden[:, :, None].to_broadcast([P, BT * HEADS, HD]), ALU.mult).then_inc(att_ready, 1)
                yield B_SUM
                dve.wait_ge(proj_ready, b + 1)
                nc.vector.tensor_tensor(x_tok[:, b * BT:(b + 1) * BT, :], tiles(PS_A), x_tok[:, b * BT:(b + 1) * BT, :],
                                        ALU.add).then_inc(x_ready, 1)

            def route(r, b):
                yield R_STATS
                dve.wait_ge(x_ready, r + 1)
                norm_stats(route_ln, tile_of(b))
                yield R_MV
                norm_mv(route_ln, r)
                yield R_Z
                norm(route_ln, r, zr, tile_of(b), which=range(BT // 2))
                yield R_Z + 1
                norm(route_ln, r, zr, tile_of(b), which=range(BT // 2, BT))
                yield R_GUARD
                dve.wait_ge(logits_ready, r + 1)
                x = logit[:, 3, :]
                nc.vector.tensor_copy(x, ps[:, PS_B, 0:BT * E]).then_inc(logit_out, 1)
                dve.wait_ge(logit_out, LOGIT_STEPS * r + 1)
                nc.vector.scalar_tensor_tensor(out=logit[:, 0, :], in0=x, scalar=-1.0, in1=x,
                                               op0=ALU.mult, op1=ALU.min).then_inc(logit_out, 1)
                nc.vector.tensor_scalar(positive[:, :], x, 0.0, None, ALU.is_gt).then_inc(logit_out, 1)
                dve.wait_ge(logit_out, LOGIT_STEPS * r + 2)
                nc.vector.tensor_scalar(logit[:, 1, :], logit[:, 0, :], -TINY, None, ALU.min).then_inc(logit_out, 1)
                dve.wait_ge(logit_out, LOGIT_STEPS * r + 4)
                nc.vector.reciprocal(logit[:, 2, :], logit[:, 1, :]).then_inc(logit_out, 1)
                yield R_RANK[0]
                dve.wait_ge(scores_ready, r + 1)
                dve.wait_ge(logit_out, LOGIT_STEPS * (r + 1))
                done = [0]

                def step(ins):
                    done[0] += 1
                    ins.then_inc(route_step, 1)

                def after(n):
                    dve.wait_ge(route_step, r * ROUTE_STEPS + n)

                def tt(o, a, b, op):
                    step(nc.vector.tensor_tensor(o, a, b, op))

                tt(half_sig[:, 0, :], silu_logit[:, :], logit[:, 2, :], ALU.mult)
                after(1)
                tt(half_sig[:, 1, :], positive[:, :], half_sig[:, 0, :], ALU.subtract)
                after(2)
                step(nc.vector.scalar_tensor_tensor(out=scores[:, :, :].rearrange("p t e -> p (t e)"), in0=half_sig[:, 1, :],
                                                    scalar=-1.0, in1=half_sig[:, 1, :], op0=ALU.mult, op1=ALU.max))
                yield R_RANK[1]
                after(3)
                tt(sfc[:, :, :], scores[:, :, :], bias_route[:, None, :].to_broadcast([P, BT, E]), ALU.add)
                after(4)
                pairs = sfc[:, :, :].rearrange("p t (g two) -> p (t g) two", two=2)
                tt(pair_hi[:, :], pairs[:, :, 0], pairs[:, :, 1], ALU.max)
                tt(pair_lo[:, :], pairs[:, :, 0], pairs[:, :, 1], ALU.min)
                hi2 = pair_hi[:, :].rearrange("p (g two) -> p g two", two=2)
                lo2 = pair_lo[:, :].rearrange("p (g two) -> p g two", two=2)
                after(6)
                tt(quad[:, 0, :], hi2[:, :, 0], hi2[:, :, 1], ALU.max)
                tt(quad[:, 1, :], hi2[:, :, 0], hi2[:, :, 1], ALU.min)
                tt(quad[:, 2, :], lo2[:, :, 0], lo2[:, :, 1], ALU.max)
                yield R_RANK[2]
                after(9)
                tt(quad[:, 3, :], quad[:, 1, :], quad[:, 2, :], ALU.max)
                after(10)
                tt(quad[:, 4, :], quad[:, 0, :], quad[:, 3, :], ALU.add)
                after(11)
                gs = quad[:, 4, :].rearrange("p (t g) -> p t g", t=BT)
                tt(beats_g[:, :, :, :], gs[:, :, None, :].to_broadcast([P, BT, GROUPS, GROUPS]),
                   gs[:, :, :, None].to_broadcast([P, BT, GROUPS, GROUPS]), ALU.is_ge)
                after(12)
                tt(beats_g[:, :, :, :], beats_g[:, :, :, :],
                   lower_g[:, None, :, :].to_broadcast([P, BT, GROUPS, GROUPS]), ALU.mult)
                yield R_RANK[3]
                after(13)
                step(nc.vector.tensor_reduce(rank_g[:, 0, :], beats_g[:, :, :, :].rearrange("p t i j -> p (t i) j"),
                                             AX.X, ALU.add))
                step(nc.vector.tensor_reduce(rank_g[:, 1, :].rearrange("p (t i) -> p t i", t=BT),
                                             beats_g[:, :, :, :].rearrange("p t i j -> p t j i"), AX.X, ALU.add))
                after(15)
                tt(rank_g[:, 2, :], rank_g[:, 0, :], rank_g[:, 1, :], ALU.subtract)
                after(16)
                tt(rank_g[:, 3, :].rearrange("p (t g) -> p t g", t=BT), rank_g[:, 2, :].rearrange("p (t g) -> p t g", t=BT),
                   thr_g[:, None, :].to_broadcast([P, BT, GROUPS]), ALU.is_lt)
                yield R_RANK[4]
                after(17)
                tt(masked[:, :, :].rearrange("p t (g e) -> p (t g) e", e=GE),
                   sfc[:, :, :].rearrange("p t (g e) -> p (t g) e", e=GE),
                   rank_g[:, 3, :, None].to_broadcast([P, BT * GROUPS, GE]), ALU.mult)
                after(18)
                tt(tied[:, 0, :], masked[:, :, :].rearrange("p t e -> p (t e)"), tile_inner[:, :], ALU.mult)
                for t in range(BT):
                    step(nc.vector.max(best[:, t, :], masked[:, t, :]))
                yield R_RANK[5]
                after(23)
                fourth = best[:, :, TOPK - 1:TOPK].to_broadcast([P, BT, E])
                tt(above[:, :, :], masked[:, :, :], fourth, ALU.is_gt)
                tt(level[:, :, :], masked[:, :, :], fourth, ALU.is_equal)
                after(25)
                step(nc.vector.tensor_reduce(wsum[:, 3, :], above[:, :, :], AX.X, ALU.add))
                step(nc.vector.tensor_tensor_scan(tied[:, 1, :], tile_inner[:, :], level[:, :, :].rearrange("p t e -> p (t e)"),
                                                  0.0, ALU.mult, ALU.add))
                yield R_RANK[6]
                after(27)
                tt(tied[:, 2, :].rearrange("p (t e) -> p t e", t=BT), tied[:, 1, :].rearrange("p (t e) -> p t e", t=BT),
                   wsum[:, 3, :, None].to_broadcast([P, BT, E]), ALU.add)
                after(28)
                step(nc.vector.scalar_tensor_tensor(out=tied[:, 3, :], in0=tied[:, 2, :], scalar=float(TOPK),
                                                    in1=level[:, :, :].rearrange("p t e -> p (t e)"),
                                                    op0=ALU.is_le, op1=ALU.mult))
                after(29)
                tt(chosen[:, :], tied[:, 3, :], above[:, :, :].rearrange("p t e -> p (t e)"), ALU.add)
                yield R_RANK[7]
                after(30)
                tt(masked[:, :, :], scores[:, :, :], chosen[:, :].rearrange("p (t e) -> p t e", t=BT), ALU.mult)
                after(31)
                step(nc.vector.tensor_reduce(wsum[:, 0, :], masked[:, :, :], AX.X, ALU.add))
                yield R_RANK[8]
                after(32)
                step(nc.vector.tensor_scalar(wsum[:, 1, :], wsum[:, 0, :], TOPK_EPS, None, ALU.add))
                after(33)
                step(nc.vector.reciprocal(wsum[:, 2, :], wsum[:, 1, :]))
                after(34)
                tt(cw[:, :, :], masked[:, :, :], wsum[:, 2, :, None].to_broadcast([P, BT, E]), ALU.mult)
                yield R_RANK[9]
                after(35)
                assert done[0] == ROUTE_STEPS
                left = cw[:, :, :]
                for part in range(PARTS):
                    here = cw_parts[:, :, part * E:(part + 1) * E]
                    nc.vector.tensor_copy(here, left).then_inc(cw_split, 1)
                    dve.wait_ge(cw_split, r * CW_SPLITS + 2 * part + 1)
                    if part < PARTS - 1:
                        nc.vector.tensor_tensor(cw_left[:, part, :, :], left, here, ALU.subtract).then_inc(cw_split, 1)
                        dve.wait_ge(cw_split, r * CW_SPLITS + 2 * part + 2)
                        left = cw_left[:, part, :, :]

            def fold():
                yield F_OUT
                dve.wait_ge(fold_ps, 1)
                nc.vector.tensor_copy(w_mix[:, :], fold_mix).then_inc(folded, 1)
                nc.vector.tensor_tensor(w_mix_s[:, :], fold_mix_s, w_out_s[:, :], ALU.add).then_inc(folded, 1)
                nc.vector.tensor_tensor(w_small[:, :], fold_small, w_in_s[:, :], ALU.add).then_inc(folded, 1)
                nc.vector.tensor_tensor(b_small[:, :], fold_bias, b_small_in[:, :], ALU.add).then_inc(folded, 1)
                dve.wait_ge(folded, FOLDED - 1)
                nc.vector.tensor_scalar(b_half[:, :], b_small[:, :], 0.5, None, ALU.mult).then_inc(folded, 1)

            def recur(m):
                yield M_SUM
                dve.wait_ge(y_turned, m + 1)
                nc.vector.tensor_tensor(xcur[:, :, :], tiles(PS_A), x_tok[:, ds(m * BT, BT), :], ALU.add).then_inc(xcur_ready, 1)
                yield M_STATS
                dve.wait_ge(xcur_ready, m + 1)
                norm_stats(rec_ln, lambda t: xcur[:, t, :])
                yield M_MV
                norm_mv(rec_ln, m)
                yield M_SCAN[0]
                dve.wait_ge(thT_ready, m + 1)
                nc.vector.tensor_scalar(gT, thT, 0.5, 0.5, ALU.mult, ALU.add).then_inc(scan_step, 1)
                nc.vector.tensor_scalar(omgT, thT, -0.5, 0.5, ALU.mult, ALU.add).then_inc(scan_step, 1)
                yield M_SCAN[1]
                dve.wait_ge(scan_step, SCAN_STEPS * m + 2)
                nc.vector.scalar_tensor_tensor(out=inT, in0=ps[0:SD, PS_A, :], scalar=b_small[0:SD, 0:1], in1=omgT,
                                               op0=ALU.add, op1=ALU.mult).then_inc(scan_step, 1)
                yield M_SCAN[2]
                dve.wait_ge(scan_step, SCAN_STEPS * m + 3)
                nc.vector.tensor_tensor_scan(stT[0:SD, :], gT, inT, carry[:, 0:1], ALU.mult, ALU.add).then_inc(scan_step, 1)
                dve.wait_ge(scan_step, SCAN_STEPS * m + 4)
                nc.vector.tensor_tensor(carry[:, 0:1], stT[0:SD, BLK - 1:BLK], keep[:, ds(m, 1)], ALU.mult).then_inc(scan_step, 1)
                yield M_X
                dve.wait_ge(mix_ready, m + 1)
                nc.vector.tensor_tensor(x_tok[:, ds(m * BT, BT), :], tiles(PS_A), xcur[:, :, :], ALU.add).then_inc(x_ready, 1)

            def output(o, unit=O_SUM):
                yield unit
                dve.wait_ge(y_turned, NBLK + o + 1)
                if o:
                    dve.wait_ge(out_stored, 16 * o)
                nc.vector.tensor_tensor(xcur[:, :, :], tiles(PS_A), x_tok[:, o * BT:(o + 1) * BT, :], ALU.add)\
                    .then_inc(out_ready, 1)

            def ffn(p, sides, first=False):
                for u in range(UNITS):
                    n = p * UNITS + u
                    if u >= 1 and u - 1 not in SHARED_AT:
                        if u - 1 in HALF_AT:
                            dve.wait_ge(c_ready, HALVES * p + HALF_AT.index(u - 1) + 1)
                        dve.wait_ge(act_ready, p * EU + routed_units(u))
                        if not first or u >= 3:
                            dve.wait_ge(lo_ready, freed(p, u - 1))
                        nc.vector.tensor_tensor(hid_sb[:, (u - 1) % 2, :], bank(PS_C), act_sb[:, (u - 1) % 2, :],
                                                ALU.mult).then_inc(hid_ready, 1)
                    dve.wait_ge(silu_ready, n + 1)
                    dve.wait_ge(u_ready, n + 1)
                    if u not in SHARED_AT:
                        if not first or u >= 2:
                            dve.wait_ge(hid_ready, freed(p, u))
                        dst, told = act_sb, act_ready
                    else:
                        if not first or u >= 2:
                            dve.wait_ge(lo_ready, freed(p, u))
                        dst, told = hid_sb, hid_ready
                    nc.vector.tensor_tensor(dst[:, u % 2, :], bank(PS_U[u % 2]), silu_sb[:, u % 2, :], ALU.mult).then_inc(told, 1)
                    beside(sides, u)

            for a in range(2):
                attn_stats(a)
                attn_norm(a)
            dve.wait_ge(attn_loaded, 16 * len(ATTN_IN))
            for a in range(2):
                for t in range(BT):
                    rotate(a, t)
            attn_stats(2)
            sum_kv(0)
            sum_kv(1)
            attn_norm(2)
            r0, b0, b1 = started(route(0, 0)), started(attend(0)), started(attend(1))
            beside([b0], B_DEN)
            attn_stats(3)
            rotate(2, 0)
            beside([b0], B_SUM)
            beside([r0], R_MV)
            attn_norm(3)
            beside([r0], R_Z + 1)
            for t in range(1, BT):
                rotate(2, t)
            dve.wait_ge(const_loaded, 16 * len(CONST_IN))
            dve.wait_ge(ident_ready, 1)
            beside([r0], R_GUARD)
            rotate(3, 0)
            beside([r0], R_RANK[0])
            rotate(3, 1)
            beside([r0], R_RANK[2])
            sum_kv(2)
            beside([r0], R_RANK[3])
            rotate(3, 2)
            beside([b1], B_DEN)
            rotate(3, 3)
            beside([r0], R_RANK[-1])
            beside([b1], B_SUM)
            sum_kv(3)
            ffn(0, [started(route(1, 1)), started(attend(attn_block(0)))], first=True)
            ffn(1, [started(route(2, 2)), started(attend(attn_block(1))), started(fold())])
            dve.wait_ge(folded, FOLDED)
            with dve.Fori(2, LAST_REC + 1) as p:
                ffn(p, [started(route(p + 1, (p + 1) % NBLK)), started(recur(p - 2))])
            ffn(FFN_BLOCKS - 2, [started(route(FFN_BLOCKS - 1, NBLK - 1)), started(output(0))])
            ffn(FFN_BLOCKS - 1, [started(output(1)), started(output(2, O_SUM2))])
            beside([started(output(3))], O_SUM)

        @block.tensor
        def _(pe):
            def turn(dst_bank, src):
                for t in range(BT):
                    last = nc.tensor.transpose(ps[:, dst_bank, t * P:(t + 1) * P], src(t), ident[:, :])
                return last

            def attn_turn(a):
                pe.wait_ge(attn_ln.z_ready, BT * (a + 1))
                turn(a_bank[a], lambda t: a_z[a][:, t, :]).then_inc(z_turned, 1)

            def attn_qkv(a, t):
                n = a * BT + t
                if t == 0:
                    pe.wait_ge(zT_ready, a + 1)
                if n >= BT:
                    pe.wait_ge(v_ready, n - 3 if a < 2 else n - 2)
                nc.tensor.matmul(ps[:, qkv_banks[a][t], 0:3 * D], a_zT[a][:, t * P:(t + 1) * P], w_qkv[:, :],
                                 start=True, stop=True).then_inc(qkv_ready, 1)

            def attn_kv(a):
                pe.wait_ge(qk_ready, BT * (a + 1))
                if a:
                    if a % 2:
                        pe.wait_ge(kv_out, a // 2 * 2 + 1)
                    else:
                        pe.wait_ge(kv_ready, a // 2)
                for t in range(BT):
                    last = nc.tensor.matmul(ps[:, kv_bank, 0:KVW], qk_of[a % 2][:, t, 1, :], v_of[a % 2][:, t, :],
                                            start=(t == 0), stop=(t == BT - 1))
                last.then_inc(kv_multiplied, 1)
                if a:
                    pe.wait_ge(qT_ready, a)
                for t in range(BT):
                    last = nc.tensor.transpose(ps[:, q_bank, t * P:(t + 1) * P], qk_of[a % 2][:, t, 0, :], ident[:, :])
                last.then_inc(q_turned, 1)

            def attend(b, attT):
                yield B_NUM
                pe.wait_ge(qT_ready, b + 1)
                pe.wait_ge(kv_ready, b // 2 + 1)
                if b:
                    pe.wait_ge(x_ready, b)
                    pe.wait_ge(logit_out, LOGIT_STEPS * b)
                for t in range(BT):
                    q_t = qT[:, (b * BT + t) * P:(b * BT + t + 1) * P]
                    nc.tensor.matmul(ps[:, PS_A, t * P:(t + 1) * P], q_t, kv[:, b // 2, 0:D], start=True, stop=True)
                    last = nc.tensor.matmul(ps[:, PS_B, t * HEADS:(t + 1) * HEADS], q_t, kv[:, b // 2, D:KVW],
                                            start=True, stop=True)
                last.then_inc(num_ready, 1)
                yield B_TURN
                pe.wait_ge(att_ready, b + 1)
                turn(PS_A, lambda t: xcur[:, t, :]).then_inc(att_turned, 1)
                yield B_PROJ
                pe.wait_ge(attT_ready, b + 1)
                for t in range(BT):
                    last = nc.tensor.matmul(ps[:, PS_A, t * P:(t + 1) * P], attT[:, t * P:(t + 1) * P], w_o[:, :],
                                            start=True, stop=True)
                last.then_inc(proj_ready, 1)

            def route(r, beside_done=None, first=False, turn_at=R_TURN_CW):
                yield R_TURN
                pe.wait_ge(route_ln.z_ready, BT * (r + 1))
                if not first:
                    pe.wait_ge(routed, r)
                turn(PS_B, lambda t: zr[:, t, :]).then_inc(zr_turned, 1)
                yield R_LOGIT
                pe.wait_ge(zrT_ready, r + 1)
                pe.wait_ge(xh_ready, r + 1)
                for t in range(BT):
                    last = nc.tensor.matmul(ps[:, PS_B, t * E:(t + 1) * E], zrT[:, t * P:(t + 1) * P], w_route[:, :],
                                            start=True, stop=True)
                last.then_inc(logits_ready, 1)
                yield turn_at
                pe.wait_ge(cw_split, (r + 1) * CW_SPLITS)
                if beside_done:
                    pe.wait_ge(*beside_done)
                for t in range(BT):
                    last = nc.tensor.transpose(psB_bf[:, t * P:(t + 1) * P], cw_parts[:, t, :], ident_bf[:, :])
                last.then_inc(cw_turned, 1)

            def fold():
                yield F_FOLD
                pe.wait_ge(x_ready, attn_block(1) + 1)
                nc.tensor.matmul(fold_mix, w_inT[:, :], w_out[:, :], start=True, stop=True)
                nc.tensor.matmul(fold_mix_s, b_in[:, :], w_out[:, :], start=True, stop=True)
                nc.tensor.matmul(fold_small, w_inT[:, :], w_g[:, :], start=True, stop=False)
                nc.tensor.matmul(fold_small, w_inT_s[:, :], w_g_s[:, :], start=False, stop=True)
                nc.tensor.matmul(fold_bias, w_g[:, :], b_in[:, SD:SD + 1], start=True, stop=False)
                nc.tensor.matmul(fold_bias, w_g_s[:, :], b_in_s[:, :], start=False, stop=True).then_inc(fold_ps, 1)

            def recur(m):
                yield M_TURN
                pe.wait_ge(y_out, m + 1)
                pe.wait_ge(x_ready, NBLK + m)
                turn(PS_A, lambda t: yT[:, t * P:(t + 1) * P]).then_inc(y_turned, 1)
                yield M_TURN_Z
                pe.wait_ge(rec_ln.z_ready, BT * (m + 1))
                turn(PS_A, lambda t: z[:, t, :]).then_inc(zm_turned, 1)
                yield M_GATE
                pe.wait_ge(zmT_ready, m + 1)
                nc.tensor.matmul(ps[0:SMALL, PS_A, :], w_small[:, :], zT[:, :], start=True, stop=True).then_inc(gate_ps, 1)
                yield M_MIX
                pe.wait_ge(scan_step, SCAN_STEPS * (m + 1))
                for t in range(BT):
                    cols = slice(t * P, (t + 1) * P)
                    nc.tensor.matmul(ps[:, PS_A, cols], zT[:, cols], w_mix[:, :], start=True, stop=False)
                    last = nc.tensor.matmul(ps[:, PS_A, cols], stT[:, cols], w_mix_s[:, :], start=False, stop=True)
                last.then_inc(mix_ready, 1)

            def output(o, unit=O_TURN):
                yield unit
                pe.wait_ge(y_out, NBLK + o + 1)
                if o:
                    pe.wait_ge(out_ready, o)
                else:
                    pe.wait_ge(x_ready, FFN_BLOCKS)
                turn(PS_A, lambda t: yT[:, t * P:(t + 1) * P]).then_inc(y_turned, 1)

            def times(dst, w, cols, hi, lo, start, stop):
                nc.tensor.matmul(dst, W_hi[w][:, cols], hi, start=start, stop=False)
                nc.tensor.matmul(dst, W_hi[w][:, cols], lo, start=False, stop=False)
                return nc.tensor.matmul(dst, W_lo[w][:, cols], hi, start=False, stop=stop)

            def down(u, seen):
                pe.wait_ge(lo_ready, seen)
                times(bank(PS_Y), 2, slice(u * P, (u + 1) * P), hid_hi[:, u % HBUF, :], hid_lo[:, u % HBUF, :],
                      u == 0, u == UNITS - 1).then_inc(down_done, 1)

            def ffn(p, slot, sides, first=False):
                blk = ds(slot * BLK, BLK)
                pe.wait_ge(xl_ready, p + 1)
                for u in range(UNITS):
                    cols = slice(u * P, (u + 1) * P)
                    if first and u % WCH == 0:
                        pe.wait_ge(piece_lo, 3 * (u // WCH + 1))
                    if not first or u >= 2:
                        pe.wait_ge(silu_ready, freed(p, u))
                    times(bank(PS_G[u % 2]), 0, cols, xh[:, blk], xl[:, blk], True, True).then_inc(g_ready, 1)
                    if u in HALF_AT:
                        half = HALF_AT.index(u)
                        if half == 0:
                            pe.wait_ge(routed, p + 1)
                        if half or not first:
                            pe.wait_ge(hid_ready, p * UNITS + u - 1 if half else p * UNITS - 1)
                        nc.tensor.matmul(bank(PS_C), expert_of[:, half * P:(half + 1) * P], cwT[:, blk],
                                         start=True, stop=True).then_inc(c_ready, 1)
                    if not first or u >= 2:
                        pe.wait_ge(*product_done(p, u))
                    times(bank(PS_U[u % 2]), 1, cols, xh[:, blk], xl[:, blk], True, True).then_inc(u_ready, 1)
                    if u == LAG and not first:
                        pe.wait_ge(y_out, p)
                    if u >= LAG or not first:
                        down((u - LAG) % UNITS, p * UNITS + u - LAG + 1)
                    beside(sides, u)

            pe.wait_ge(ident_ready, 2)
            attn_turn(0)
            pe.wait_ge(attn_loaded, 16 * len(ATTN_IN))
            attn_qkv(0, 0)
            attn_qkv(0, 1)
            attn_turn(1)
            attn_qkv(0, 2)
            attn_qkv(0, 3)
            for t in range(BT):
                attn_qkv(1, t)
            attn_kv(0)
            attn_kv(1)
            r0, b0, b1 = started(route(0, (den_ready, 2), first=True, turn_at=UNITS)), started(attend(0, yT)), started(attend(1, zT))
            beside([b0], B_NUM)
            attn_turn(2)
            beside([b0], B_TURN)
            attn_qkv(2, 0)
            beside([b0], B_PROJ)
            attn_qkv(2, 1)
            attn_qkv(2, 2)
            attn_turn(3)
            beside([r0], R_TURN)
            attn_qkv(2, 3)
            pe.wait_ge(const_loaded, 16 * len(CONST_IN))
            beside([r0], R_LOGIT)
            attn_qkv(3, 0)
            attn_qkv(3, 1)
            attn_kv(2)
            attn_qkv(3, 2)
            beside([b1], B_NUM)
            attn_qkv(3, 3)
            beside([b1], B_PROJ)
            attn_kv(3)
            ffn(0, 0, [started(last_step(r0)), started(route(1, (den_ready, 3))), started(attend(attn_block(0), zT))], first=True)
            ffn(1, 1, [started(route(2, (den_ready, 4))), started(attend(attn_block(1), zT)), started(fold())])
            pe.wait_ge(folded, FOLDED)
            with pe.Fori(2, LAST_REC + 1) as p:
                ffn(p, p % NBLK, [started(route(p + 1)), started(recur(p - 2))])
            ffn(FFN_BLOCKS - 2, NBLK - 2, [started(route(FFN_BLOCKS - 1)), started(output(0))])
            ffn(FFN_BLOCKS - 1, NBLK - 1, [started(output(1)), started(output(2, O_TURN2))])
            for u in range(UNITS - LAG, UNITS):
                down(u, (FFN_BLOCKS - 1) * UNITS + u + 1)
            beside([started(output(3))], O_TURN)


def kernel(**inputs):
    import numpy as np
    import ml_dtypes
    import concourse.bacc as _bacc
    from concourse import mybir as _mybir
    from concourse.bass_utils import run_bass_kernel_spmd as _run

    g = {k: np.asarray(v) for k, v in inputs.items()}
    order = np.concatenate([np.arange(0, D, 2), np.arange(1, D, 2)])

    def units(routed, shared):
        halves = routed.reshape(HALVES, EH, HU, BAND, D).transpose(0, 2, 1, 3, 4).reshape(HALVES, HU * P, D)
        full = np.zeros((HID, D), np.float32)
        for half in range(HALVES):
            at = HALF_AT[half] * P
            full[at:at + HU * P] = halves[half]
        for i, u in enumerate(SHARED_AT):
            rows = shared[i * P:(i + 1) * P]
            full[u * P:u * P + rows.shape[0]] = rows
        return full

    def beside_zeros(a, at, columns):
        full = np.zeros((a.shape[0], columns), np.float32)
        full[:, at:at + a.shape[1]] = a
        return full

    w_in = g["L0_attn_b_W_in"]
    gate = units(g["L0_ffn_gate_proj"], g["L0_ffn_shared_gate_w"]).T
    up = units(g["L0_ffn_up_proj"], g["L0_ffn_shared_up_w"]).T
    down = units(g["L0_ffn_down_proj"].transpose(0, 2, 1), g["L0_ffn_shared_down_w"].T)
    down = down.reshape(UNITS, P, D).transpose(1, 0, 2).reshape(P, HID)

    freqs = np.float32(1.0) / np.float32(10000.0) ** (np.arange(0, HD, 2, dtype=np.float32) / np.float32(HD))
    ang = (np.arange(SEQ, dtype=np.float32)[:, None] * freqs[None, :]).astype(np.float32)
    cos = np.tile(np.cos(ang).astype(np.float32), (1, HEADS)).reshape(SEQ // P, P, D // 2).transpose(1, 0, 2)
    sin = np.tile(np.sin(ang).astype(np.float32), (1, HEADS)).reshape(SEQ // P, P, D // 2).transpose(1, 0, 2)
    head = np.arange(D // 2) // (HD // 2)
    head = np.concatenate([head, head])
    value_head = np.concatenate([np.arange(D) // HD, np.arange(HEADS)])
    expert_of = np.zeros((P, HALVES * P), np.float32)
    for part in range(PARTS):
        expert_of[part * E + np.arange(HALVES * P) // BAND, np.arange(HALVES * P)] = 1.0
    rows = {
        "x": g["L0_attn_a_x"].reshape(BATCH * SEQ, D),
        "w_qkv": np.concatenate([g["L0_attn_a_Wq"][:, order], g["L0_attn_a_Wk"][:, order], g["L0_attn_a_Wv"]], axis=1),
        "w_o": g["L0_attn_a_Wo"],
        "head_mask": (head[:, None] == value_head[None, :]).astype(np.float32),
        "cos": cos,
        "sin": np.stack([sin, -sin], axis=2),
        "w_route": g["L0_ffn_gate_w"].T,
        "bias_route": np.repeat(g["L0_ffn_gate_bias"][None, :], P, axis=0),
        "tile_inner": np.repeat((np.arange(BT * E) % E != 0).astype(np.float32)[None, :], P, axis=0),
        "thr_g": np.repeat(np.arange(GROUPS, dtype=np.float32)[None, :] - (GROUPS - 1 - TOPG), P, axis=0),
        "lower_g": np.repeat(np.tril(np.ones((GROUPS, GROUPS), np.float32), -1)[None], P, axis=0),
        "w_inT": w_in[:, :D].T,
        "w_inT_s": w_in[:, D:].T,
        "w_in_s": beside_zeros(w_in[:, D:], 0, SMALL),
        "b_in": beside_zeros(g["L0_attn_b_b_in"][:D, None], SD, SD + 1),
        "b_in_s": g["L0_attn_b_b_in"][D:, None],
        "w_g": beside_zeros(g["L0_attn_b_W_g"][:D], GATE_AT, SMALL),
        "w_g_s": beside_zeros(g["L0_attn_b_W_g"][D:], GATE_AT, SMALL),
        "b_small_in": np.concatenate([g["L0_attn_b_b_in"][D:], np.zeros(GATE_AT - SD, np.float32),
                                      g["L0_attn_b_b_g"]])[:, None],
        "w_out": g["L0_attn_b_W_out"][:D],
        "w_out_s": np.concatenate([g["L0_attn_b_W_out"][D:], g["L0_attn_b_b_out"][None, :]], axis=0),
        "keep": np.repeat((np.arange(1, NBLK + 1) % (SEQ // BLK) != 0).astype(np.float32)[None, :], SD, axis=0),
        "expert_of": expert_of.astype(ml_dtypes.bfloat16),
        "gate_proj": gate,
        "up_proj": up,
        "down_proj": down,
    }
    nc = _bacc.Bacc("TRN2", target_bir_lowering=False, num_devices=1)
    arrays, args = {}, {}
    for name, a in rows.items():
        a = np.ascontiguousarray(a)
        arrays[f"{name}_dram"] = a
        args[name] = nc.dram_tensor(f"{name}_dram", a.shape, _mybir.dt.from_np(a.dtype), kind="ExternalInput").ap()
    out = nc.dram_tensor("out_dram", (BATCH * SEQ, D), _mybir.dt.float32, kind="ExternalOutput").ap()
    hybrid_kernel(nc, args, out)
    r = _run(nc, [arrays], core_ids=[0])
    return r.results[0]["out_dram"].reshape(BATCH, SEQ, D)
```
